# Optimizing a Trainium2 kernel written in Bass

```python
import numpy as np
import jax
import jax.numpy as jnp

def _softmax(x, axis=-1):
    return jax.nn.softmax(x, axis=axis)

def _gelu(x):
    return jax.nn.gelu(x, approximate=True)

def _silu(x):
    return jax.nn.silu(x)

def _sigmoid(x):
    return jax.nn.sigmoid(x)

def _layernorm(x, axis=-1, eps=1e-05):
    m = jnp.mean(x, axis=axis, keepdims=True)
    v = jnp.var(x, axis=axis, keepdims=True)
    return (x - m) / jnp.sqrt(v + eps)

def _scatter_add(tgt, idx, src, axis=0):
    return tgt.at[idx].add(src)

def _segment_sum(src, seg, n):
    return jax.ops.segment_sum(src, seg, n)
kernel_name = 'mk_xattn_seq_d4_seqx_r4_974c2d'

def setup_inputs(seed: int=0):
    np.random.seed(seed)
    _w = jnp.asarray

    def _rec_inputs():
        import jax
        import jax.numpy as jnp
        _rk = jax.random.key(seed)
        x = -0.0002928 + 1 * jax.random.normal(jax.random.fold_in(_rk, 1), (4, 1024, 256), jnp.float32)
        _lenS = 1024 - jax.random.randint(jax.random.fold_in(_rk, 7), (4,), 0, max(1, 1024 // 4) + 1, jnp.int32)
        _lenS2 = 77 - jax.random.randint(jax.random.fold_in(_rk, 8), (4,), 0, max(1, 77 // 4) + 1, jnp.int32)
        _ctx_1024P = jax.random.normal(jax.random.fold_in(_rk, 11), (4, 16, 256), jnp.float32)
        _ctx_1024c = jax.random.dirichlet(jax.random.fold_in(_rk, 511), 0.3 * jnp.ones((16,), jnp.float32), (4, 77))
        _ctx_1024t = jnp.einsum('bsk,bkd->bsd', _ctx_1024c, _ctx_1024P)
        _ctx_1024t = _ctx_1024t * jax.lax.rsqrt(jnp.mean(jnp.square(_ctx_1024t)) + 1e-12) * 0.953939
        ctx_1024 = -1.39393e-06 + 0.999914 * (_ctx_1024t + 0.3 * jax.random.normal(jax.random.fold_in(_rk, 611), (4, 77, 256), jnp.float32))
        _validS = jnp.arange(1024)[None, :] < _lenS[:, None]
        _validS2 = jnp.arange(77)[None, :] < _lenS2[:, None]
        _causal = jnp.tril(jnp.ones((1024, 1024), dtype=bool))
        mask_1x1xSxS_bk0 = jnp.logical_not(jnp.broadcast_to(_validS[0:1, None, None, :], (1, 1, 1024, 1024)))
        return (x, ctx_1024, mask_1x1xSxS_bk0)
    x, ctx_1024, mask_1x1xSxS_bk0 = _rec_inputs()

    def _L0_xattn_setup():
        import jax, jax.numpy as jnp
        import numpy as np
        EMBED_DIM = 256
        NUM_HEADS = 16
        HEAD_DIM = EMBED_DIM // NUM_HEADS
        FF_DIM = 1024
        B, T, S = (2, 512, 512)
        LN_EPS = 1e-05

        def _layernorm(x, g, b):
            mu = jnp.mean(x, -1, keepdims=True)
            var = jnp.mean(jnp.square(x - mu), -1, keepdims=True)
            return (x - mu) * jax.lax.rsqrt(var + LN_EPS) * g + b

        def _mha(q_in, k_in, v_in, wq, bq, wk, bk, wv, bv, wo, bo, mask=None):
            Bq, Tq, C = q_in.shape
            Tk = k_in.shape[1]
            Q = (q_in @ wq + bq).reshape(Bq, Tq, NUM_HEADS, HEAD_DIM)
            K = (k_in @ wk + bk).reshape(Bq, Tk, NUM_HEADS, HEAD_DIM)
            V = (v_in @ wv + bv).reshape(Bq, Tk, NUM_HEADS, HEAD_DIM)
            scores = jnp.einsum('bqhd,bkhd->bhqk', Q, K) / np.sqrt(HEAD_DIM)
            if mask is not None:
                scores = jnp.where(mask, scores, -jnp.inf)
            attn = jax.nn.softmax(scores, axis=-1)
            out = jnp.einsum('bhqk,bkhd->bqhd', attn, V).reshape(Bq, Tq, C)
            return out @ wo + bo
        key = jax.random.key(seed)
        ks = jax.random.split(key, 20)
        sd = 1.0 / np.sqrt(EMBED_DIM)
        d = {'x': jax.random.normal(ks[0], (B, T, EMBED_DIM), jnp.float32), 'encoder_outputs': jax.random.normal(ks[1], (B, S, EMBED_DIM), jnp.float32), 'tgt_mask': jnp.tril(jnp.ones((T, T), bool))[None, None]}
        names = ['sa_wq', 'sa_wk', 'sa_wv', 'sa_wo', 'ca_wq', 'ca_wk', 'ca_wv', 'ca_wo']
        for i, n in enumerate(names):
            d[n] = jax.random.normal(ks[2 + i], (EMBED_DIM, EMBED_DIM), jnp.float32) * sd
            d[n.replace('w', 'b')] = jnp.zeros((EMBED_DIM,), jnp.float32)
        d['ff_w1'] = jax.random.normal(ks[10], (EMBED_DIM, FF_DIM), jnp.float32) * sd
        d['ff_b1'] = jnp.zeros((FF_DIM,), jnp.float32)
        d['ff_w2'] = jax.random.normal(ks[11], (FF_DIM, EMBED_DIM), jnp.float32) * (1.0 / np.sqrt(FF_DIM))
        d['ff_b2'] = jnp.zeros((EMBED_DIM,), jnp.float32)
        for i in (1, 2, 3):
            d[f'ln{i}_g'] = jnp.ones((EMBED_DIM,), jnp.float32)
            d[f'ln{i}_b'] = jnp.zeros((EMBED_DIM,), jnp.float32)
        return d
    _L0_xattn_all = _L0_xattn_setup()
    _L0_xattn_in = {k: v for k, v in _L0_xattn_all.items() if k in ('sa_wq', 'sa_bq', 'sa_wk', 'sa_bk', 'sa_wv', 'sa_bv', 'sa_wo', 'sa_bo', 'ca_wq', 'ca_bq', 'ca_wk', 'ca_bk', 'ca_wv', 'ca_bv', 'ca_wo', 'ca_bo', 'ff_w1', 'ff_b1', 'ff_w2', 'ff_b2', 'ln1_g', 'ln1_b', 'ln2_g', 'ln2_b', 'ln3_g', 'ln3_b')}
    del _L0_xattn_all

    def _L1_xattn_setup():
        import jax, jax.numpy as jnp
        import numpy as np
        NEG = -4294967295.0
        EPS = 1e-08
        H = 4
        L = 3

        def _layer_norm(x, g, b):
            mean = jnp.mean(x, axis=-1, keepdims=True)
            std = jnp.std(x, axis=-1, keepdims=True, ddof=1)
            return g * (x - mean) / (std + EPS) + b

        def _mha_layer(q, k, v, Wq, bq, Wk, bk, Wv, bv, gamma, beta):
            B, Sq, d = q.shape
            Sk = k.shape[1]
            dh = d // H
            Q = jax.nn.relu(q @ Wq + bq)
            K = jax.nn.relu(k @ Wk + bk)
            V = jax.nn.relu(v @ Wv + bv)
            Qh = Q.reshape(B, Sq, H, dh).transpose(2, 0, 1, 3)
            Kh = K.reshape(B, Sk, H, dh).transpose(2, 0, 1, 3)
            Vh = V.reshape(B, Sk, H, dh).transpose(2, 0, 1, 3)
            scores = jnp.einsum('hbqd,hbkd->hbqk', Qh, Kh) / jnp.sqrt(jnp.float32(dh))
            key_mask = jnp.sign(jnp.abs(jnp.sum(k, axis=-1)))
            scores = jnp.where(key_mask[None, :, None, :] == 0.0, NEG, scores)
            attn = jax.nn.softmax(scores, axis=-1)
            query_mask = jnp.sign(jnp.abs(jnp.sum(q, axis=-1)))
            attn = attn * query_mask[None, :, :, None]
            out = jnp.einsum('hbqk,hbkd->hbqd', attn, Vh)
            out = out.transpose(1, 2, 0, 3).reshape(B, Sq, d)
            out = out + q
            return _layer_norm(out, gamma, beta)
        key = jax.random.key(seed)
        ks = jax.random.split(key, 8)
        B, S, d = (2, 512, 256)
        inp = {'queries': jax.random.normal(ks[0], (B, S, d), jnp.float32), 'keys': jax.random.normal(ks[1], (B, S, d), jnp.float32), 'values': jax.random.normal(ks[2], (B, S, d), jnp.float32), 'Wq': jax.random.normal(ks[3], (L, d, d), jnp.float32) * 0.02, 'bq': jnp.zeros((L, d), jnp.float32), 'Wk': jax.random.normal(ks[4], (L, d, d), jnp.float32) * 0.02, 'bk': jnp.zeros((L, d), jnp.float32), 'Wv': jax.random.normal(ks[5], (L, d, d), jnp.float32) * 0.02, 'bv': jnp.zeros((L, d), jnp.float32), 'gamma': jnp.ones((L, d), jnp.float32), 'beta': jnp.zeros((L, d), jnp.float32), 'Wff': jax.random.normal(ks[6], (L, d, d), jnp.float32) * 0.02, 'bff': jnp.zeros((L, d), jnp.float32)}
        return inp
    _L1_xattn_all = _L1_xattn_setup()
    _L1_xattn_in = {k: v for k, v in _L1_xattn_all.items() if k in ('Wq', 'bq', 'Wk', 'bk', 'Wv', 'bv', 'gamma', 'beta', 'Wff', 'bff')}
    del _L1_xattn_all

    def _L2_xattn_setup():
        import jax, jax.numpy as jnp
        import numpy as np
        D_MODEL = 256
        N_HEADS = 16
        D_K = D_MODEL // N_HEADS
        EPS = 1e-05

        def _split_heads(x, B):
            S = x.shape[1]
            return x.reshape(B, S, N_HEADS, D_K).transpose(0, 2, 1, 3)
        key = jax.random.key(seed)
        ks = jax.random.split(key, 14)
        B, S, D = (4, 512, D_MODEL)
        s = 1.0 / np.sqrt(D)
        return {'q': jax.random.normal(ks[0], (B, S, D), jnp.float32), 'k': jax.random.normal(ks[1], (B, S, D), jnp.float32), 'v': jax.random.normal(ks[2], (B, S, D), jnp.float32), 'Wq': jax.random.normal(ks[3], (D, D), jnp.float32) * s, 'bq': jnp.zeros((D,), jnp.float32), 'Wk': jax.random.normal(ks[4], (D, D), jnp.float32) * s, 'bk': jnp.zeros((D,), jnp.float32), 'Wv': jax.random.normal(ks[5], (D, D), jnp.float32) * s, 'bv': jnp.zeros((D,), jnp.float32), 'Wo': jax.random.normal(ks[6], (D, D), jnp.float32) * s, 'bo': jnp.zeros((D,), jnp.float32), 'gamma': jnp.ones((D,), jnp.float32), 'beta': jnp.zeros((D,), jnp.float32)}
    _L2_xattn_all = _L2_xattn_setup()
    _L2_xattn_in = {k: v for k, v in _L2_xattn_all.items() if k in ('Wq', 'bq', 'Wk', 'bk', 'Wv', 'bv', 'Wo', 'bo', 'gamma', 'beta')}
    del _L2_xattn_all

    def _L3_xattn_setup():
        import jax, jax.numpy as jnp
        import numpy as np
        H = 16
        D = 256
        DK = D // H
        key = jax.random.key(seed)
        ks = jax.random.split(key, 10)
        B, S = (2, 512)
        scale = 1.0 / np.sqrt(D)
        inp = {'query': jax.random.normal(ks[0], (B, S, D), jnp.float32), 'key_': jax.random.normal(ks[1], (B, S, D), jnp.float32), 'value': jax.random.normal(ks[2], (B, S, D), jnp.float32), 'Wq': jax.random.normal(ks[3], (D, D), jnp.float32) * scale, 'bq': jnp.zeros((D,), jnp.float32), 'Wk': jax.random.normal(ks[4], (D, D), jnp.float32) * scale, 'bk': jnp.zeros((D,), jnp.float32), 'Wv': jax.random.normal(ks[5], (D, D), jnp.float32) * scale, 'bv': jnp.zeros((D,), jnp.float32), 'ln_gamma': jnp.ones((D,), jnp.float32), 'ln_beta': jnp.zeros((D,), jnp.float32)}
        return inp
    _L3_xattn_all = _L3_xattn_setup()
    _L3_xattn_in = {k: v for k, v in _L3_xattn_all.items() if k in ('Wq', 'bq', 'Wk', 'bk', 'Wv', 'bv', 'ln_gamma', 'ln_beta')}
    del _L3_xattn_all
    return {'x': x, 'ctx_1024': ctx_1024, 'mask_1x1xSxS_bk0': mask_1x1xSxS_bk0, 'L0_xattn_sa_wq': _L0_xattn_in['sa_wq'], 'L0_xattn_sa_bq': _L0_xattn_in['sa_bq'], 'L0_xattn_sa_wk': _L0_xattn_in['sa_wk'], 'L0_xattn_sa_bk': _L0_xattn_in['sa_bk'], 'L0_xattn_sa_wv': _L0_xattn_in['sa_wv'], 'L0_xattn_sa_bv': _L0_xattn_in['sa_bv'], 'L0_xattn_sa_wo': _L0_xattn_in['sa_wo'], 'L0_xattn_sa_bo': _L0_xattn_in['sa_bo'], 'L0_xattn_ca_wq': _L0_xattn_in['ca_wq'], 'L0_xattn_ca_bq': _L0_xattn_in['ca_bq'], 'L0_xattn_ca_wk': _L0_xattn_in['ca_wk'], 'L0_xattn_ca_bk': _L0_xattn_in['ca_bk'], 'L0_xattn_ca_wv': _L0_xattn_in['ca_wv'], 'L0_xattn_ca_bv': _L0_xattn_in['ca_bv'], 'L0_xattn_ca_wo': _L0_xattn_in['ca_wo'], 'L0_xattn_ca_bo': _L0_xattn_in['ca_bo'], 'L0_xattn_ff_w1': _L0_xattn_in['ff_w1'], 'L0_xattn_ff_b1': _L0_xattn_in['ff_b1'], 'L0_xattn_ff_w2': _L0_xattn_in['ff_w2'], 'L0_xattn_ff_b2': _L0_xattn_in['ff_b2'], 'L0_xattn_ln1_g': _L0_xattn_in['ln1_g'], 'L0_xattn_ln1_b': _L0_xattn_in['ln1_b'], 'L0_xattn_ln2_g': _L0_xattn_in['ln2_g'], 'L0_xattn_ln2_b': _L0_xattn_in['ln2_b'], 'L0_xattn_ln3_g': _L0_xattn_in['ln3_g'], 'L0_xattn_ln3_b': _L0_xattn_in['ln3_b'], 'L1_xattn_Wq': _L1_xattn_in['Wq'], 'L1_xattn_bq': _L1_xattn_in['bq'], 'L1_xattn_Wk': _L1_xattn_in['Wk'], 'L1_xattn_bk': _L1_xattn_in['bk'], 'L1_xattn_Wv': _L1_xattn_in['Wv'], 'L1_xattn_bv': _L1_xattn_in['bv'], 'L1_xattn_gamma': _L1_xattn_in['gamma'], 'L1_xattn_beta': _L1_xattn_in['beta'], 'L1_xattn_Wff': _L1_xattn_in['Wff'], 'L1_xattn_bff': _L1_xattn_in['bff'], 'L2_xattn_Wq': _L2_xattn_in['Wq'], 'L2_xattn_bq': _L2_xattn_in['bq'], 'L2_xattn_Wk': _L2_xattn_in['Wk'], 'L2_xattn_bk': _L2_xattn_in['bk'], 'L2_xattn_Wv': _L2_xattn_in['Wv'], 'L2_xattn_bv': _L2_xattn_in['bv'], 'L2_xattn_Wo': _L2_xattn_in['Wo'], 'L2_xattn_bo': _L2_xattn_in['bo'], 'L2_xattn_gamma': _L2_xattn_in['gamma'], 'L2_xattn_beta': _L2_xattn_in['beta'], 'L3_xattn_Wq': _L3_xattn_in['Wq'], 'L3_xattn_bq': _L3_xattn_in['bq'], 'L3_xattn_Wk': _L3_xattn_in['Wk'], 'L3_xattn_bk': _L3_xattn_in['bk'], 'L3_xattn_Wv': _L3_xattn_in['Wv'], 'L3_xattn_bv': _L3_xattn_in['bv'], 'L3_xattn_ln_gamma': _L3_xattn_in['ln_gamma'], 'L3_xattn_ln_beta': _L3_xattn_in['ln_beta']}

def reference(x, ctx_1024, mask_1x1xSxS_bk0, L0_xattn_sa_wq, L0_xattn_sa_bq, L0_xattn_sa_wk, L0_xattn_sa_bk, L0_xattn_sa_wv, L0_xattn_sa_bv, L0_xattn_sa_wo, L0_xattn_sa_bo, L0_xattn_ca_wq, L0_xattn_ca_bq, L0_xattn_ca_wk, L0_xattn_ca_bk, L0_xattn_ca_wv, L0_xattn_ca_bv, L0_xattn_ca_wo, L0_xattn_ca_bo, L0_xattn_ff_w1, L0_xattn_ff_b1, L0_xattn_ff_w2, L0_xattn_ff_b2, L0_xattn_ln1_g, L0_xattn_ln1_b, L0_xattn_ln2_g, L0_xattn_ln2_b, L0_xattn_ln3_g, L0_xattn_ln3_b, L1_xattn_Wq, L1_xattn_bq, L1_xattn_Wk, L1_xattn_bk, L1_xattn_Wv, L1_xattn_bv, L1_xattn_gamma, L1_xattn_beta, L1_xattn_Wff, L1_xattn_bff, L2_xattn_Wq, L2_xattn_bq, L2_xattn_Wk, L2_xattn_bk, L2_xattn_Wv, L2_xattn_bv, L2_xattn_Wo, L2_xattn_bo, L2_xattn_gamma, L2_xattn_beta, L3_xattn_Wq, L3_xattn_bq, L3_xattn_Wk, L3_xattn_bk, L3_xattn_Wv, L3_xattn_bv, L3_xattn_ln_gamma, L3_xattn_ln_beta):
    import jax
    import jax.numpy as jnp

    def _L0_xattn_ref(x, encoder_outputs, tgt_mask, sa_wq, sa_bq, sa_wk, sa_bk, sa_wv, sa_bv, sa_wo, sa_bo, ca_wq, ca_bq, ca_wk, ca_bk, ca_wv, ca_bv, ca_wo, ca_bo, ff_w1, ff_b1, ff_w2, ff_b2, ln1_g, ln1_b, ln2_g, ln2_b, ln3_g, ln3_b):
        import jax, jax.numpy as jnp
        import numpy as np
        EMBED_DIM = 256
        NUM_HEADS = 16
        HEAD_DIM = EMBED_DIM // NUM_HEADS
        FF_DIM = 1024
        B, T, S = (2, 512, 512)
        LN_EPS = 1e-05

        def _layernorm(x, g, b):
            mu = jnp.mean(x, -1, keepdims=True)
            var = jnp.mean(jnp.square(x - mu), -1, keepdims=True)
            return (x - mu) * jax.lax.rsqrt(var + LN_EPS) * g + b

        def _mha(q_in, k_in, v_in, wq, bq, wk, bk, wv, bv, wo, bo, mask=None):
            Bq, Tq, C = q_in.shape
            Tk = k_in.shape[1]
            Q = (q_in @ wq + bq).reshape(Bq, Tq, NUM_HEADS, HEAD_DIM)
            K = (k_in @ wk + bk).reshape(Bq, Tk, NUM_HEADS, HEAD_DIM)
            V = (v_in @ wv + bv).reshape(Bq, Tk, NUM_HEADS, HEAD_DIM)
            scores = jnp.einsum('bqhd,bkhd->bhqk', Q, K) / np.sqrt(HEAD_DIM)
            if mask is not None:
                scores = jnp.where(mask, scores, -jnp.inf)
            attn = jax.nn.softmax(scores, axis=-1)
            out = jnp.einsum('bhqk,bkhd->bqhd', attn, V).reshape(Bq, Tq, C)
            return out @ wo + bo
        h = _layernorm(x, ln1_g, ln1_b)
        x = x + _mha(h, h, h, sa_wq, sa_bq, sa_wk, sa_bk, sa_wv, sa_bv, sa_wo, sa_bo, tgt_mask)
        h = _layernorm(x, ln2_g, ln2_b)
        x = x + _mha(h, encoder_outputs, encoder_outputs, ca_wq, ca_bq, ca_wk, ca_bk, ca_wv, ca_bv, ca_wo, ca_bo, None)
        h = _layernorm(x, ln3_g, ln3_b)
        ff = jax.nn.relu(h @ ff_w1 + ff_b1) @ ff_w2 + ff_b2
        return x + ff

    def _L1_xattn_ref(queries, keys, values, Wq, bq, Wk, bk, Wv, bv, gamma, beta, Wff, bff):
        import jax, jax.numpy as jnp
        import numpy as np
        NEG = -4294967295.0
        EPS = 1e-08
        H = 4
        L = 3

        def _layer_norm(x, g, b):
            mean = jnp.mean(x, axis=-1, keepdims=True)
            std = jnp.std(x, axis=-1, keepdims=True, ddof=1)
            return g * (x - mean) / (std + EPS) + b

        def _mha_layer(q, k, v, Wq, bq, Wk, bk, Wv, bv, gamma, beta):
            B, Sq, d = q.shape
            Sk = k.shape[1]
            dh = d // H
            Q = jax.nn.relu(q @ Wq + bq)
            K = jax.nn.relu(k @ Wk + bk)
            V = jax.nn.relu(v @ Wv + bv)
            Qh = Q.reshape(B, Sq, H, dh).transpose(2, 0, 1, 3)
            Kh = K.reshape(B, Sk, H, dh).transpose(2, 0, 1, 3)
            Vh = V.reshape(B, Sk, H, dh).transpose(2, 0, 1, 3)
            scores = jnp.einsum('hbqd,hbkd->hbqk', Qh, Kh) / jnp.sqrt(jnp.float32(dh))
            key_mask = jnp.sign(jnp.abs(jnp.sum(k, axis=-1)))
            scores = jnp.where(key_mask[None, :, None, :] == 0.0, NEG, scores)
            attn = jax.nn.softmax(scores, axis=-1)
            query_mask = jnp.sign(jnp.abs(jnp.sum(q, axis=-1)))
            attn = attn * query_mask[None, :, :, None]
            out = jnp.einsum('hbqk,hbkd->hbqd', attn, Vh)
            out = out.transpose(1, 2, 0, 3).reshape(B, Sq, d)
            out = out + q
            return _layer_norm(out, gamma, beta)
        q, k, v = (queries, keys, values)
        enc = q
        for i in range(L):
            enc = _mha_layer(q, k, v, Wq[i], bq[i], Wk[i], bk[i], Wv[i], bv[i], gamma[i], beta[i])
            enc = jax.nn.leaky_relu(enc @ Wff[i] + bff[i], negative_slope=0.2) + enc
            q, k, v = (enc, enc, enc)
        return enc

    def _L2_xattn_ref(q, k, v, Wq, bq, Wk, bk, Wv, bv, Wo, bo, gamma, beta):
        import jax, jax.numpy as jnp
        import numpy as np
        D_MODEL = 256
        N_HEADS = 16
        D_K = D_MODEL // N_HEADS
        EPS = 1e-05

        def _split_heads(x, B):
            S = x.shape[1]
            return x.reshape(B, S, N_HEADS, D_K).transpose(0, 2, 1, 3)
        B = q.shape[0]
        residual = q
        qh = _split_heads(q @ Wq.T + bq, B)
        kh = _split_heads(k @ Wk.T + bk, B)
        vh = _split_heads(v @ Wv.T + bv, B)
        scale = jnp.asarray(D_MODEL, q.dtype) ** 0.5
        scores = jnp.einsum('bhsd,bhtd->bhst', qh / scale, kh)
        attn = jax.nn.softmax(scores, axis=-1)
        out = jnp.einsum('bhst,bhtd->bhsd', attn, vh)
        out = out.transpose(0, 2, 1, 3).reshape(B, -1, D_MODEL)
        out = out @ Wo.T + bo
        x = out + residual
        mu = jnp.mean(x, axis=-1, keepdims=True)
        var = jnp.var(x, axis=-1, keepdims=True)
        return (x - mu) * jax.lax.rsqrt(var + EPS) * gamma + beta

    def _L3_xattn_ref(query, key_, value, Wq, bq, Wk, bk, Wv, bv, ln_gamma, ln_beta):
        import jax, jax.numpy as jnp
        import numpy as np
        H = 16
        D = 256
        DK = D // H
        B, S, _ = query.shape
        residual = query

        def proj(x, W, b):
            return (x @ W + b).reshape(B, -1, H, DK).transpose(0, 2, 1, 3)
        q = proj(query, Wq, bq)
        k = proj(key_, Wk, bk)
        v = proj(value, Wv, bv)
        scores = jnp.einsum('bhqd,bhkd->bhqk', q, k) / jnp.sqrt(jnp.float32(DK))
        p_att = jax.nn.softmax(scores, axis=-1)
        x = jnp.einsum('bhqk,bhkd->bhqd', p_att, v)
        x = x.transpose(0, 2, 1, 3).reshape(B, S, D)
        y = x + residual
        mu = jnp.mean(y, axis=-1, keepdims=True)
        var = jnp.var(y, axis=-1, keepdims=True)
        y = (y - mu) / jnp.sqrt(var + 1e-06)
        return y * ln_gamma + ln_beta
    x = _L0_xattn_ref(x, ctx_1024, mask_1x1xSxS_bk0, L0_xattn_sa_wq, L0_xattn_sa_bq, L0_xattn_sa_wk, L0_xattn_sa_bk, L0_xattn_sa_wv, L0_xattn_sa_bv, L0_xattn_sa_wo, L0_xattn_sa_bo, L0_xattn_ca_wq, L0_xattn_ca_bq, L0_xattn_ca_wk, L0_xattn_ca_bk, L0_xattn_ca_wv, L0_xattn_ca_bv, L0_xattn_ca_wo, L0_xattn_ca_bo, L0_xattn_ff_w1, L0_xattn_ff_b1, L0_xattn_ff_w2, L0_xattn_ff_b2, L0_xattn_ln1_g, L0_xattn_ln1_b, L0_xattn_ln2_g, L0_xattn_ln2_b, L0_xattn_ln3_g, L0_xattn_ln3_b)
    x = _L1_xattn_ref(x, ctx_1024, ctx_1024, L1_xattn_Wq, L1_xattn_bq, L1_xattn_Wk, L1_xattn_bk, L1_xattn_Wv, L1_xattn_bv, L1_xattn_gamma, L1_xattn_beta, L1_xattn_Wff, L1_xattn_bff)
    x = _L2_xattn_ref(x, ctx_1024, ctx_1024, L2_xattn_Wq, L2_xattn_bq, L2_xattn_Wk, L2_xattn_bk, L2_xattn_Wv, L2_xattn_bv, L2_xattn_Wo, L2_xattn_bo, L2_xattn_gamma, L2_xattn_beta)
    x = _L3_xattn_ref(x, ctx_1024, ctx_1024, L3_xattn_Wq, L3_xattn_bq, L3_xattn_Wk, L3_xattn_bk, L3_xattn_Wv, L3_xattn_bv, L3_xattn_ln_gamma, L3_xattn_ln_beta)
    return x

_drawn_inputs = setup_inputs


def setup_inputs(seed=0):
    import zlib

    import numpy as np

    out = dict(_drawn_inputs(seed))
    spreads = {'L0_xattn_sa_bq': (0.0, 0.329),
     'L0_xattn_sa_bk': (0.0, 2.0),
     'L0_xattn_sa_bv': (0.0, 0.1),
     'L0_xattn_sa_bo': (0.0, 0.1),
     'L0_xattn_ca_bq': (0.0, 0.582),
     'L0_xattn_ca_bk': (0.0, 2.0),
     'L0_xattn_ca_bv': (0.0, 0.1),
     'L0_xattn_ca_bo': (0.0, 0.1),
     'L0_xattn_ff_b1': (0.0, 0.1),
     'L0_xattn_ff_b2': (0.0, 0.1),
     'L0_xattn_ln1_g': (1.0, 0.2),
     'L0_xattn_ln1_b': (0.0, 0.1),
     'L0_xattn_ln2_g': (1.0, 0.558),
     'L0_xattn_ln2_b': (0.0, 0.525),
     'L0_xattn_ln3_g': (1.0, 0.2),
     'L0_xattn_ln3_b': (0.0, 0.1),
     'L1_xattn_bq': (0.0, 0.8),
     'L1_xattn_bk': (0.0, 0.8),
     'L1_xattn_bv': (0.0, 0.1),
     'L1_xattn_gamma': (1.0, 0.2),
     'L1_xattn_beta': (0.0, 0.1),
     'L1_xattn_bff': (0.0, 0.1),
     'L2_xattn_bq': (0.0, 2.0),
     'L2_xattn_bk': (0.0, 2.0),
     'L2_xattn_bv': (0.0, 0.1),
     'L2_xattn_bo': (0.0, 0.1),
     'L2_xattn_gamma': (1.0, 0.2),
     'L2_xattn_beta': (0.0, 0.1),
     'L3_xattn_bq': (0.0, 0.396),
     'L3_xattn_bk': (0.0, 2.0),
     'L3_xattn_bv': (0.0, 0.1),
     'L3_xattn_ln_gamma': (1.0, 0.2),
     'L3_xattn_ln_beta': (0.0, 0.1)}
    factors = {'L1_xattn_Wq': 8.0, 'L1_xattn_Wk': 8.0}
    for name, (base, spread) in spreads.items():
        noise = np.random.default_rng([zlib.crc32(name.encode()), seed]).standard_normal(out[name].shape)
        drawn = base * np.exp(spread * noise) if base else spread * noise
        out[name] = jnp.asarray(drawn.astype(out[name].dtype))
    for name, factor in factors.items():
        out[name] = (out[name] * factor).astype(out[name].dtype)
    return out
```

```python
from contextlib import ExitStack

import concourse.bass as bass
from concourse import mybir

F32 = mybir.dt.float32
F32R = mybir.dt.float32r
BF16 = mybir.dt.bfloat16
U8 = mybir.dt.uint8
I32 = mybir.dt.int32
ALU = mybir.AluOpType
ACT = mybir.ActivationFunctionType
AX = mybir.AxisListType

P = 128
B, T, D = 4, 1024, 256
C = 77
TILES = T // P
HALF = 512
FH = D // P
FF = 4 * D
BIG = 1e30
LOWEST = -1e29
NEG = -4294967295.0
PAD = 64
RING = [0, 1, 2, 3, 6]
KM, ACC, DEN = 0, 6, 7
QM_RING = {16: [4, 5, 7], 64: [4, 5]}
SETS = 3
LEAD = {16: 5, 64: 3}
PAIR = {16: 2, 64: 1}
STACK_DMAS = {16: 4, 64: 4}
PBUFS = 6


class Attention:
    def __init__(self, number, dh, own, relu, masked, scale):
        self.number, self.dh, self.own, self.relu, self.masked, self.scale = number, dh, own, relu, masked, scale
        self.keyed = relu
        self.heads = D // dh


ATTENTIONS = [Attention(0, 16, True, False, True, 0.25), Attention(1, 16, False, False, False, 0.25),
              Attention(2, 64, False, True, False, 0.125), Attention(3, 64, True, True, False, 0.125),
              Attention(4, 64, True, True, False, 0.125), Attention(5, 16, False, False, False, 1.0 / 16),
              Attention(6, 16, False, False, False, 0.25)]

UNIT = FH * D
PHASE_UNITS = [4, 4, 8, 4, 4, 4, 4, 3]
PHASE_AT = [sum(PHASE_UNITS[:i]) * UNIT for i in range(8)]
ROWS = 4
LN_COL = [0, 2, 4]
FF_COL = 6
QK_COL = 10
VECTORS = QK_COL + 2 * len(ATTENTIONS)


class Counts:
    def __init__(self):
        self.job = self.act = self.dve = self.kq = 0
        self.slot = self.exp = self.turn = 0
        self.qm = self.m = self.placed = 0
        self.joined = 0
        self.pv = self.acc = 0
        self.ln = self.xn = self.x = self.xb = 0
        self.bd = self.ms = self.pads = self.sums = 0
        self.stacked = (0,) * SETS
        self.phase = 0


class Step:
    def __init__(self, n, kind, a=None, by=None, bank=0, reuse=None, free=None, first=False, last=False,
                 g=0, c=0, hl=0, half=0, pair=0, head=0, t=0, tile=0, f=0, side="", source="", scaled=None,
                 part=0, row=0, into="", eps=None, own=False, buf=0, units=None):
        self.kind, self.a, self.by, self.bank, self.reuse, self.free = kind, a, by, bank, reuse, free
        self.first, self.last, self.g, self.c, self.hl, self.half, self.pair = first, last, g, c, hl, half, pair
        self.head, self.t, self.tile, self.f, self.side, self.source, self.scaled = head, t, tile, f, side, source, scaled
        self.part, self.row, self.into, self.eps, self.own, self.buf, self.units = part, row, into, eps, own, buf, units
        self.job, self.act, self.dve, self.kq, self.slot, self.exp = n.job, n.act, n.dve, n.kq, n.slot, n.exp
        self.turn, self.qm, self.m, self.placed, self.pv, self.acc = n.turn, n.qm, n.m, n.placed, n.pv, n.acc
        self.ln, self.xn, self.x, self.xb, self.bd, self.ms = n.ln, n.xn, n.x, n.xb, n.bd, n.ms
        self.pads, self.sums, self.stacked, self.phase, self.joined = n.pads, n.sums, n.stacked, n.phase, n.joined
        self.pv_before = 0


def schedule():
    steps = []
    n = Counts()
    jobs = {0: (0, 0)}
    slots = {}

    def put(kind, **place):
        steps.append(Step(n, kind, **place))

    def job(kind, by, **kw):
        n.job += 1
        n.act += by == "act"
        n.dve += by in ("dve", "both")
        n.kq += by == "both"
        jobs[n.job] = (n.act, n.dve)
        put(kind, by=by, bank=RING[(n.job - 1) % len(RING)], reuse=jobs.get(n.job - len(RING), (0, 0)), **kw)

    def turn_in(source, scaled=None, xn=0):
        for half in range(2):
            for f in range(FH):
                job("to_features", "act", source=source, scaled=scaled, half=half, f=f)

    def norm(kind, eps):
        n.ln += 1
        put("norm", into=kind, eps=eps)
        n.xn += TILES * (kind == "features")
        n.x += TILES * (kind == "x")

    def take_slot():
        n.slot += 1
        return slots.get(n.slot - 2, (0, 0))

    def attend(a):
        put("begin_attention", a=a)
        n.pads += 1
        put("pads", a=a)
        if not a.relu and a.number < 6:
            n.xb += 1
            put("bias_x", row=1)
        if a.own:
            self_attention(a)
        else:
            cross_attention(a)
        put("end_attention", a=a)

    def km(a, **kw):
        free = take_slot()
        n.exp += 1
        slots[n.slot] = (n.exp, n.turn)
        put("km", a=a, free=free, buf=(n.exp - 1) % PBUFS, **kw)


    def pv(a, last, units, **kw):
        n.pv += 1
        n.acc += last
        for u in units:
            pv_of_exp[u] = n.pv
        put("pv", a=a, last=last, units=units, **kw)

    def turn(a, **kw):
        free = take_slot()
        n.turn += 1
        slots[n.slot] = (n.exp, n.turn)
        put("turn", a=a, free=free, **kw)

    def take_qm_bank(a):
        if a not in qm_banks:
            qm_banks.clear()
            qm_banks[a] = []
        used, ring = qm_banks[a], QM_RING[a.dh]
        return used, dict(bank=ring[len(used) % len(ring)],
                          free=used[-len(ring)] if len(used) >= len(ring) else (0, 0))

    def qm(a, **kw):
        used, place = take_qm_bank(a)
        n.qm += 1
        used.append((n.qm, 0))
        put("qm", a=a, **place, **kw)

    def m(a, **kw):
        used, place = take_qm_bank(a)
        n.m += 1
        used.append((0, n.m))
        put("m", a=a, **place, **kw)
        if a.own:
            n.placed += 16 * PAIR[a.dh]

    qm_banks = {}

    def stack(a, g):
        dmas = 16 * PAIR[a.dh] * STACK_DMAS[a.dh]
        n.stacked = tuple(c + dmas * (i == g % SETS) for i, c in enumerate(n.stacked))
        put("stack", a=a, g=g)

    pv_of_exp = {}

    def kq(a, side, f, half):
        job("project_kq", "both", a=a, side=side, f=f, half=half)

    def v(a, t):
        job("project_v", "dve", a=a, t=t)

    def self_attention(a):
        per = PAIR[a.dh]
        groups = a.heads // per
        units = TILES * per
        for half in range(2):
            kq(a, "k", 0, half)
        for half in range(2):
            kq(a, "q", 0, half)
        for g in range(SETS):
            if g * per * a.dh < P:
                stack(a, g)
        exp0 = n.exp
        maxima = iter([(g, i) for g in range(groups) for i in range(units)])

        def take_maxima(tiles=1):
            for _ in range(tiles):
                g, i = next(maxima, (0, None))
                if i is not None:
                    for half in range(2):
                        qm(a, g=g, tile=i, half=half)
                    if i == units - 1:
                        n.joined += 1
                        put("join", a=a, g=g)

        rest = [("v", t) for t in range(TILES)] + [(s, h) for s in "kq" for h in range(2)]
        for i, (what, x) in enumerate(rest):
            if what == "v":
                v(a, x)
            else:
                kq(a, what, 1, x)
            if i >= 4:
                take_maxima()
        for g in range(SETS):
            if g * per * a.dh >= P:
                stack(a, g)
        take_maxima(units + LEAD[a.dh] - (len(rest) - 4))
        m(a, g=0)
        for g in range(groups):
            for i in range(units):
                c, hl = divmod(i, per)
                km(a, g=g, c=c, hl=hl, head=g * per + hl, first=i == 0)
                take_maxima()
                if hl == per - 1:
                    if c == 0 and g > 0:
                        pv(a, True, [exp0 + g * units - k for k in range(per)][::-1], g=g - 1, c=TILES - 1)
                    if c >= 1:
                        pv(a, False, [exp0 + g * units + (c - 1) * per + k + 1 for k in range(per)], g=g, c=c - 1)
                    if c == 2 and g > 0:
                        turn(a, g=g - 1)
                if i == units - LEAD[a.dh] + 1 and g + 1 < groups:
                    m(a, g=g + 1)
                if i == units - 1 and g + SETS < groups:
                    stack(a, g + SETS)
        pv(a, True, [n.exp - k for k in range(per)][::-1], g=groups - 1, c=TILES - 1)
        turn(a, g=groups - 1)

    def cross_attention(a):
        for f in range(FH):
            kq(a, "k", f, 0)
        v(a, 0)
        for f in range(FH):
            kq(a, "q", f, 0)
        n.bd += 1
        put("spread_keys", a=a)
        per = 8 if a.dh == 16 else 2
        group = 4 if a.dh == 16 else 2
        halves = 2 if a.dh == 16 else 1

        def take_maxima(t, f):
            for half in range(halves):
                qm(a, tile=t, f=f, half=half)

        for t in range(4):
            for f in range(FH):
                take_maxima(t, f)
        for f in range(FH):
            kq(a, "q", f, 1)
        n.ms += 1
        m(a, half=0)
        later = iter([(t, f) for t in range(4, 8) for f in range(FH)])
        each = 8 // (a.heads // 2)
        pending = None
        for half in range(2):
            for g in range(a.heads // group):
                units = []
                for s in range(group // 2):
                    km(a, half=half, pair=(g * group) // 2 + s, first=half + g + s == 0)
                    units.append(n.exp)
                    if half == 0:
                        for _ in range(each):
                            t, f = next(later)
                            take_maxima(t, f)
                if pending:
                    turn(a, **pending)
                pv(a, True, units, half=half, g=g)
                pending = dict(half=half, g=g)
            if half == 0:
                n.ms += 1
                m(a, half=1)
        turn(a, **pending)

    def phase(number):
        n.phase = number
        put("phase")

    def next_phase():
        put("phase_end")

    put("load")
    job("to_features_ctx", "act")
    for p in range(2):
        phase(p)
        norm("features", 1e-5)
        turn_in("xn", LN_COL[p])
        attend(ATTENTIONS[p])
        turn_in("attended")
        for t in range(TILES):
            job("add_projected", "dve", t=t)
        next_phase()
    phase(2)
    norm("features", 1e-5)
    turn_in("xn", LN_COL[2])
    n.xb += 1
    put("bias_x", row=0)
    for f in range(FF // P):
        for half in range(2):
            job("hidden", "act", f=f, half=half)
    for t in range(TILES):
        job("add_hidden", "dve", t=t)
    next_phase()
    for p in range(3, 6):
        phase(p)
        n.sums += 1
        put("sums", own=p > 3)
        if p > 3:
            job("key_row", "act", part=0)
            job("key_row", "act", part=1)
        turn_in("x")
        attend(ATTENTIONS[p - 1])
        n.x += 1
        put("add_attended")
        norm("x", None)
        turn_in("x")
        for t in range(TILES):
            job("leaky", "dve", t=t)
        next_phase()
    phase(6)
    turn_in("x")
    attend(ATTENTIONS[5])
    turn_in("attended")
    for t in range(TILES):
        job("add_projected", "dve", t=t)
    norm("x", 1e-5)
    next_phase()
    phase(7)
    turn_in("x")
    attend(ATTENTIONS[6])
    n.x += 1
    put("add_attended")
    norm("x", 1e-6)
    next_phase()
    put("store")
    for s in steps:
        if s.kind == "km":
            s.pv_before = pv_of_exp.get(s.exp - PBUFS, 0)
    return steps


def attention_stack(nc, x, ctx_in, mask, mask_t, weights, rows, vectors, out):
    steps = schedule()
    stacks_at = {(s.a, s.g): s.stacked[s.g % SETS] for s in steps if s.kind == "stack"}
    joined_at = {(s.a, s.g): s.joined for s in steps if s.kind == "join"}
    ctx = ExitStack()
    with ctx:
        def sb(name, shape, dt=F32):
            return ctx.enter_context(nc.sbuf_tensor(name, shape, dt))

        def sem(name):
            cleared_each_batch.append(ctx.enter_context(nc.semaphore(name)))
            return cleared_each_batch[-1]

        cleared_each_batch = []
        X = sb("X", [P, TILES, D])
        XN = sb("XN", [P, TILES, D])
        HT = sb("HT", [P, FH, T])
        QK = sb("QK", [P, 4, FH, T], F32R)
        VP = sb("VP", [P, 4096 + PBUFS * T])
        STACK = sb("STACK", [P, 4 * SETS, T], F32R)
        MASK_Q = sb("MASK_Q", [P, TILES, T], BF16)
        MASK_K = sb("MASK_K", [P, TILES, T], BF16)
        W = [sb("W_even", [P, 8 * UNIT]), sb("W_odd", [P, 4 * UNIT])]
        R = [sb("R_even", [P, ROWS, D]), sb("R_odd", [P, ROWS, D])]
        KEY_ROW = sb("KEY_ROW", [P, T], BF16)
        CT = sb("CT", [P, FH, C])
        COL = sb("COL", [P, FH, VECTORS])
        ACCS = sb("ACCS", [P, 2, HALF])
        CX = ACCS[0:C, 0, 0:D]
        TMP = sb("TMP", [P, HALF])
        VEC = TMP[0:VECTORS, 0:D]
        ident = sb("ident", [P, P])
        ident_bf = sb("ident_bf", [P, P], BF16)
        ones = sb("ones", [P, P])
        block16 = sb("block16", [P, 8])
        block64 = sb("block64", [P, 2])
        of_head = sb("of_head", [P, 16])
        half_power = sb("half_power", [P, 2, TILES])
        stats = sb("stats", [P, TILES, 6])
        mv = sb("mv", [P, TILES, 2])
        var = sb("var", [P, TILES])
        rstd = sb("rstd", [P, TILES])
        M = sb("M", [P, 2, 2, 16])
        MJ = sb("MJ", [P, 2, 16])
        MC = sb("MC", [P, TILES, 16])
        MT = sb("MT", [P, 2, P], F32R)
        MTC = TMP[:, 0:P]
        REC = sb("REC", [P, 16])
        SUM = sb("SUM", [P, 16])
        rowsum = sb("rowsum", [P, TILES])
        qmask = sb("qmask", [P, TILES])
        kneg = sb("kneg", [P, TILES])
        kneg_raw = sb("kneg_raw", [P, TILES])
        csum = sb("csum", [C, 1])
        cneg = sb("cneg", [C, 1])
        cneg_raw = sb("cneg_raw", [C, 1])
        cdiag = sb("cdiag", [C, 2, C], F32R)
        diag = TMP[:, :].rearrange("p (t n) -> p t n", t=4)
        PS = ctx.enter_context(nc.psum_tensor("PS", [P, 8, HALF], F32))

        V = VP[:, 0:4096]
        V16 = V.rearrange("p (c h e) -> p c h e", h=16, e=32)
        V64 = VP[:, 0:TILES * D].rearrange("p (c n) -> p c n", c=TILES)
        PR = VP[:, 4096:4096 + PBUFS * T].rearrange("p (u n) -> p u n", u=PBUFS)
        HID = VP[:, 0:FF // P * T].rearrange("p (f n) -> p f n", f=FF // P)
        WORDS = VP[:, 0:2 * TILES * T // 4].bitcast(I32).rearrange("p (a t n) -> p a t n", a=2, t=TILES)
        RAW = VP[:, 0:2 * TILES * T // 4].bitcast(U8).rearrange("p (a t n) -> p a t n", a=2, t=TILES)
        KBD = STACK[:, 0:4, :].rearrange("p a n -> p (a n)")[:, 0:4 * 8 * C].rearrange(
            "p (a f h k) -> p a f h k", a=2, f=FH, h=8)
        MS = STACK[:, 4, :].rearrange("p (a n) -> p a n", a=2)
        OF_HEAD = STACK[:, 5:7, :].rearrange("p a n -> p (a n)")[:, 0:16 * C].rearrange("p (h k) -> p h k", h=16)
        DUMP = TMP[:, :].bitcast(BF16)

        loaded = sem("loaded")
        weights_in = [sem("weights_even"), sem("weights_odd")]
        job_filled = sem("job_filled")
        act_emptied = sem("act_emptied")
        dve_emptied = sem("dve_emptied")
        hi_written = sem("hi_written")
        xn_ready = sem("xn_ready")
        x_ready = sem("x_ready")
        var_ready = sem("var_ready")
        rstd_ready = sem("rstd_ready")
        x_biased = sem("x_biased")
        pads_set = sem("pads_set")
        stacked = [sem(f"stacked_{i}") for i in range(SETS)]
        qm_filled = sem("qm_filled")
        qm_reduced = sem("qm_reduced")
        m_joined = sem("m_joined")
        m_turned = sem("m_turned")
        m_written = sem("m_written")
        m_placed = sem("m_placed")
        km_filled = sem("km_filled")
        exp_done = sem("exp_done")
        pv_done = sem("pv_done")
        acc_filled = sem("acc_filled")
        acc_copied = sem("acc_copied")
        turned = sem("turned")
        attended = sem("attended")
        keys_spread = sem("keys_spread")
        m_spread = sem("m_spread")
        sums_done = sem("sums_done")
        diag_done = sem("diag_done")
        phase_done = sem("phase_done")
        dve_chain = sem("dve_chain")
        pool_chain = sem("pool_chain")
        stored = sem("stored")
        constants = ctx.enter_context(nc.semaphore("constants"))
        set_up = ctx.enter_context(nc.semaphore("set_up"))
        masks_in = ctx.enter_context(nc.semaphore("masks_in"))
        vectors_in = ctx.enter_context(nc.semaphore("vectors_in"))
        vectors_turned = ctx.enter_context(nc.semaphore("vectors_turned"))
        ended = ctx.enter_context(nc.semaphore("ended"))
        cleared = ctx.enter_context(nc.semaphore("cleared"))
        CONSTANTS = 1

        block = ctx.enter_context(nc.Block())

        def w(s, unit, k, lo, hi):
            base = unit * UNIT + k * D
            return W[s.phase % 2][:, base + lo:base + hi]

        def wait_weights(engine, s):
            engine.wait_ge(weights_in[s.phase % 2], 32 * (s.phase // 2 + 1))

        def r(s, row, parts=P):
            return R[s.phase % 2][0:parts, row, :]

        @block.sync
        def _(sp):
            sp.dma_start(VEC[:, :], vectors).then_inc(vectors_in, 16)
            sp.dma_start(WORDS[:, 0], mask.rearrange("(t p) n -> p t n", p=P)).then_inc(masks_in, 16)
            sp.dma_start(WORDS[:, 1], mask_t.rearrange("(t p) n -> p t n", p=P)).then_inc(masks_in, 16)
            with nc.sync.Fori(0, B) as b:
                def load_weights(phase):
                    lo, size = PHASE_AT[phase], PHASE_UNITS[phase] * UNIT
                    sp.dma_start(W[phase % 2][:, 0:size], weights[:, lo:lo + size])\
                        .then_inc(weights_in[phase % 2], 16)
                    sp.dma_start(R[phase % 2][:, :, :], rows[phase:phase + 1].to_broadcast([P, ROWS, D]))\
                        .then_inc(weights_in[phase % 2], 16)

                for s in steps:
                    if s.kind == "phase_end" and s.phase + 2 < 8:
                        sp.wait_ge(phase_done, s.phase + 1)
                        load_weights(s.phase + 2)
                    elif s.kind == "load":
                        sp.dma_start(X[:, :, :], x[b].rearrange("(t p) d -> p t d", p=P)).then_inc(loaded, 16)
                        sp.dma_start(CX[:, :], ctx_in[b]).then_inc(loaded, 16)
                        load_weights(0)
                        load_weights(1)
                    elif s.kind == "stack":
                        a, g = s.a, s.g
                        per = PAIR[a.dh]
                        f = g * per * a.dh // P
                        sp.wait_ge(dve_emptied, s.dve)
                        if g < SETS:
                            sp.wait_ge(pads_set, s.pads)
                        else:
                            sp.wait_ge(km_filled, s.exp)
                        for hl in range(per):
                            head = g * per + hl
                            lo = head * a.dh % P
                            q_parts, k_parts = (QK[lo:lo + a.dh, i:i + 2, f, :].bitcast(F32) for i in (0, 2))
                            if a.dh == 16:
                                k_plane, q_plane = (
                                    STACK[:, 2 * (g % SETS * 2 + hl) + i, :].bitcast(F32) for i in range(2))
                                for i in range(2):
                                    sp.dma_start(k_plane[32 * i:32 * i + 32, :], k_parts).then_inc(stacked[g % SETS], 16)
                                    sp.dma_start(q_plane[32 * i:32 * i + 32, :],
                                                 q_parts[:, i:i + 1, :].to_broadcast([16, 2, T]))\
                                        .then_inc(stacked[g % SETS], 16)
                            else:
                                planes = [STACK[:, 4 * (g % SETS) + i, :].bitcast(F32) for i in range(4)]
                                for to, part in ((planes[0], k_parts),
                                                 (planes[1], q_parts[:, 0:1, :].to_broadcast([64, 2, T])),
                                                 (planes[2][0:64, :], k_parts[:, 0, :]),
                                                 (planes[3][0:64, :], q_parts[:, 1, :])):
                                    sp.dma_start(to, part).then_inc(stacked[g % SETS], 16)
                    elif s.kind == "m" and s.a.own:
                        sp.wait_ge(m_written, s.m)
                        for hl in range(PAIR[s.a.dh]):
                            if s.a.dh == 16:
                                row = STACK[96:97, 2 * (s.g % SETS * 2 + hl) + 1, :]
                            else:
                                row = STACK[64:65, 4 * (s.g % SETS) + 3, :]
                            sp.dma_start(row.bitcast(F32).rearrange("p (t n) -> p t n", t=TILES),
                                         MT[hl * TILES:(hl + 1) * TILES, s.m % 2, :].bitcast(F32)).then_inc(m_placed, 16)
                    elif s.kind == "store":
                        sp.wait_ge(x_ready, s.x)
                        sp.dma_start(out[b].rearrange("(t p) d -> p t d", p=P), X[:, :, :]).then_inc(stored, 16)
                sp.wait_ge(stored, 16)
                sp.wait_ge(ended, 4 * b + 4)
                sp.sem_inc(stored, 1)
                for semaphore in cleared_each_batch:
                    sp.sem_clear(semaphore)
                sp.sem_inc(cleared, 1)

        @block.gpsimd
        def _(pool):
            made = [0]

            def then(ins):
                made[0] += 1
                ins.then_inc(set_up, 1)
                pool.wait_ge(set_up, made[0])

            then(nc.gpsimd.memset(ident[:, :], 0.0))
            then(nc.gpsimd.affine_select(out=ident[:, :], in_=ident[:, :], compare_op=ALU.not_equal, fill=1.0,
                                         base=0, pattern=[[-1, P]], channel_multiplier=1))
            then(nc.gpsimd.tensor_copy(ident_bf[:, :], ident[:, :]))
            then(nc.gpsimd.memset(ones[:, :], 1.0))
            then(nc.gpsimd.memset(half_power[:, 0, :], -0.5))
            then(nc.gpsimd.memset(half_power[:, 1, :], 0.5))
            then(nc.gpsimd.memset(MC[:, :, :], 0.0))
            for tile, width in ((block16, 16), (block64, 64)):
                cols = P // width
                then(nc.gpsimd.memset(tile[:, :], 1.0))
                then(nc.gpsimd.affine_select(out=tile[:, :], in_=tile[:, :], compare_op=ALU.is_ge, fill=0.0,
                                             base=0, pattern=[[-width, cols]], channel_multiplier=1))
                then(nc.gpsimd.affine_select(out=tile[:, :], in_=tile[:, :], compare_op=ALU.is_ge, fill=0.0,
                                             base=width - 1, pattern=[[width, cols]], channel_multiplier=-1))
            then(nc.gpsimd.memset(of_head[:, :], 0.0))
            for t in range(8):
                then(nc.gpsimd.affine_select(out=of_head[:, :], in_=of_head[:, :], compare_op=ALU.not_equal,
                                             fill=1.0, base=-16 * t, pattern=[[-1, 16]], channel_multiplier=1))
            nc.gpsimd.drain().then_inc(constants, 1)

            with nc.gpsimd.Fori(0, B) as b:
                links = [0]

                def link(ins):
                    links[0] += 1
                    ins.then_inc(pool_chain, 1)
                    pool.wait_ge(pool_chain, links[0])

                for s in steps:
                    if s.kind == "norm":
                        pool.wait_ge(var_ready, s.ln)
                        nc.gpsimd.tensor_tensor(rstd[:, :], var[:, :], half_power[:, 1 if s.eps is None else 0, :],
                                                ALU.pow).then_inc(rstd_ready, 1)
                        pool.wait_ge(rstd_ready, s.ln)
                    elif s.kind == "bias_x":
                        pool.wait_ge(xn_ready, s.xn)
                        pool.wait_ge(job_filled, s.job)
                        wait_weights(pool, s)
                        nc.gpsimd.tensor_tensor(
                            X[:, :, :], X[:, :, :], R[s.phase % 2][:, s.row:s.row + 1, :].to_broadcast([P, TILES, D]),
                            ALU.add).then_inc(x_biased, 1)
                        pool.wait_ge(x_biased, s.xb)
                    elif s.kind == "pads":
                        pool.wait_ge(job_filled, s.job)
                        if s.a.own and s.a.dh == 16:
                            for plane in range(4 * SETS):
                                if plane % 2 == 0:
                                    link(nc.gpsimd.memset(STACK[PAD:97, plane, :].bitcast(F32), 1.0))
                                else:
                                    link(nc.gpsimd.memset(STACK[PAD:96, plane, :].bitcast(F32), 0.0))
                        elif s.a.own:
                            for slot in range(SETS):
                                link(nc.gpsimd.memset(STACK[64:96, 4 * slot + 2, :].bitcast(F32), 1.0))
                                link(nc.gpsimd.memset(STACK[64:96, 4 * slot + 3, :].bitcast(F32), 0.0))
                        if s.a.dh == 16:
                            link(nc.gpsimd.memset(V16[:, 0:TILES if s.a.own else 1, :, 16:32], 1.0))
                        nc.gpsimd.drain().then_inc(pads_set, 1)
                nc.gpsimd.drain().then_inc(ended, 1)
                pool.wait_ge(cleared, b + 1)

        @block.tensor
        def _(pe):
            pe.wait_ge(constants, CONSTANTS)
            pe.wait_ge(vectors_in, 16)
            for f in range(FH):
                last = nc.tensor.transpose(PS[:, 0, f * VECTORS:(f + 1) * VECTORS], VEC[:, f * P:(f + 1) * P],
                                           ident[0:VECTORS, 0:VECTORS])
            last.then_inc(vectors_turned, 1)
            pe.wait_ge(vectors_turned, 2)
            pe.wait_ge(masks_in, 33)
            with nc.tensor.Fori(0, B) as b:
                for s in steps:
                    k = s.kind
                    if s.reuse is not None:
                        if s.reuse[0]:
                            pe.wait_ge(act_emptied, s.reuse[0])
                        if s.reuse[1]:
                            pe.wait_ge(dve_emptied, s.reuse[1])
                        bank = PS[:, s.bank, :]
                    if k == "phase":
                        wait_weights(pe, s)
                    elif k == "begin_attention":
                        pe.wait_ge(act_emptied, s.act)
                        if s.dve:
                            pe.wait_ge(dve_emptied, s.dve)
                    elif k == "end_attention":
                        pe.wait_ge(attended, s.turn)
                    elif k == "to_features_ctx":
                        pe.wait_ge(loaded, 32)
                        for f in range(FH):
                            last = nc.tensor.transpose(bank[:, f * C:(f + 1) * C], CX[:, f * P:(f + 1) * P],
                                                       ident[0:C, 0:C])
                        last.then_inc(job_filled, 1)
                    elif k == "to_features":
                        source = X if s.source == "x" else XN
                        for i in range(4):
                            t = 4 * s.half + i
                            if s.source == "xn":
                                pe.wait_ge(xn_ready, s.xn - TILES + t + 1)
                            elif i == 0 and s.source == "x":
                                pe.wait_ge(dve_emptied, s.dve)
                                if s.x:
                                    pe.wait_ge(x_ready, s.x)
                            last = nc.tensor.transpose(bank[:, i * P:(i + 1) * P], source[:, t, s.f * P:(s.f + 1) * P],
                                                       ident[:, :])
                        last.then_inc(job_filled, 1)
                    elif k == "key_row":
                        pe.wait_ge(diag_done, 4 * (2 * (s.phase - 4) + s.part + 1))
                        for i in range(4):
                            last = nc.tensor.matmul(bank[:, i * P:(i + 1) * P], ones[:, :], diag[:, i, :],
                                                    start=True, stop=True)
                        last.then_inc(job_filled, 1)
                    elif k == "project_kq":
                        own = s.side == "q" or s.a.own
                        n = HALF if own else C
                        for i in range(FH):
                            src = HT[:, i, s.half * HALF:(s.half + 1) * HALF] if own else CT[:, i, :]
                            last = nc.tensor.matmul(bank[:, 0:n], w(s, 0 if s.side == "q" else 1, i, s.f * P, s.f * P + P),
                                                    src, start=i == 0, stop=i == FH - 1)
                        last.then_inc(job_filled, 1)
                    elif k == "project_v":
                        n = P if s.a.own else C
                        for i in range(FH):
                            src = HT[:, i, s.t * P:(s.t + 1) * P] if s.a.own else CT[:, i, :]
                            last = nc.tensor.matmul(bank[0:n, 0:D], src, w(s, 2, i, 0, D), start=i == 0, stop=i == FH - 1)
                        last.then_inc(job_filled, 1)
                    elif k in ("add_projected", "leaky"):
                        if s.t == 0:
                            pe.wait_ge(act_emptied, s.act)
                        for i in range(FH):
                            last = nc.tensor.matmul(bank[:, 0:D], HT[:, i, s.t * P:(s.t + 1) * P], w(s, 3, i, 0, D),
                                                    start=i == 0, stop=i == FH - 1)
                        last.then_inc(job_filled, 1)
                    elif k == "hidden":
                        if s.f == 0 and s.half == 0:
                            pe.wait_ge(act_emptied, s.act - 1)
                        for i in range(FH):
                            last = nc.tensor.matmul(bank, W[0][:, i * FF + s.f * P:i * FF + (s.f + 1) * P],
                                                    HT[:, i, s.half * HALF:(s.half + 1) * HALF],
                                                    start=i == 0, stop=i == FH - 1)
                        last.then_inc(job_filled, 1)
                    elif k == "add_hidden":
                        if s.t == 0:
                            pe.wait_ge(act_emptied, s.act)
                        for i in range(FF // P):
                            base = 4 * UNIT + i * D
                            last = nc.tensor.matmul(bank[:, 0:D], HID[:, i, s.t * P:(s.t + 1) * P],
                                                    W[0][:, base:base + D], start=i == 0, stop=i == FF // P - 1)
                        last.then_inc(job_filled, 1)
                    elif k == "qm":
                        if s.free[0]:
                            pe.wait_ge(qm_reduced, s.free[0])
                        if s.free[1]:
                            pe.wait_ge(m_written, s.free[1])
                        if s.a.own:
                            if s.tile == 0 and s.half == 0:
                                pe.wait_ge(stacked[s.g % SETS], stacks_at[s.a, s.g])
                                if s.g == 0:
                                    pe.wait_ge(pads_set, s.pads)
                            if s.a.dh == 16:
                                hl, t = divmod(s.tile, TILES)
                                base = 2 * (s.g % SETS * 2 + hl)
                                kk, qq = STACK[0:96, base, :], STACK[0:96, base + 1, t * P:(t + 1) * P]
                            else:
                                kk = STACK[:, 4 * (s.g % SETS), :]
                                qq = STACK[:, 4 * (s.g % SETS) + 1, s.tile * P:(s.tile + 1) * P]
                            last = nc.tensor.matmul(PS[:, s.bank, :], qq, kk[:, s.half * HALF:(s.half + 1) * HALF],
                                                    start=True, stop=True)
                        else:
                            if s.tile == 0:
                                pe.wait_ge(keys_spread, s.bd)
                            if s.f == 0 and s.half == 0 and s.tile == 4:
                                pe.wait_ge(dve_emptied, s.dve)
                            qq = QK[:, 0, s.f, s.tile * P:(s.tile + 1) * P]
                            if s.a.dh == 16:
                                last = nc.tensor.matmul(
                                    PS[:, s.bank, 0:4 * C], qq,
                                    KBD[:, 0, s.f, 4 * s.half:4 * s.half + 4, :].rearrange("p h k -> p (h k)"),
                                    start=True, stop=True)
                            else:
                                nc.tensor.matmul(PS[:, s.bank, 0:2 * C], qq,
                                                 KBD[:, 0, s.f, 0:2, :].rearrange("p h k -> p (h k)"),
                                                 start=True, stop=False)
                                last = nc.tensor.matmul(PS[:, s.bank, 0:2 * C], ones[0:C, :].bitcast(F32R),
                                                        cdiag[:, :, :].rearrange("p h k -> p (h k)"),
                                                        start=False, stop=True)
                        last.then_inc(qm_filled, 1)
                    elif k == "m":
                        if s.free[0]:
                            pe.wait_ge(qm_reduced, s.free[0])
                        if s.free[1]:
                            pe.wait_ge(m_written, s.free[1])
                        if s.a.own:
                            pe.wait_ge(m_joined, joined_at[s.a, s.g])
                            cols = 2 * TILES if s.a.dh == 16 else TILES
                            last = nc.tensor.transpose(PS[0:cols, s.bank, 0:P], MJ[:, s.g % 2, 0:cols], ident[:, :])
                        else:
                            pe.wait_ge(qm_reduced, s.qm)
                            last = nc.tensor.transpose(PS[:, s.bank, 0:P], MC[:, :, :].rearrange("p t h -> p (t h)"),
                                                       ident[:, :])
                        last.then_inc(m_turned, 1)
                    elif k == "km":
                        if s.free[0]:
                            pe.wait_ge(exp_done, s.free[0])
                        if s.free[1]:
                            pe.wait_ge(attended, s.free[1])
                        if s.first:
                            pe.wait_ge(act_emptied, s.act)
                            pe.wait_ge(dve_emptied, s.dve)
                        bank = KM + 2 * ((s.slot - 1) % 2)
                        if s.a.own:
                            if s.first:
                                pe.wait_ge(m_placed, s.placed)
                                if s.a.dh == 64 and s.g == 0:
                                    pe.wait_ge(pads_set, s.pads)
                            if s.a.dh == 16:
                                base = 2 * (s.g % SETS * 2 + s.hl)
                                passes = [(STACK[0:97, base, s.c * P:(s.c + 1) * P], STACK[0:97, base + 1, :])]
                                if s.a.masked:
                                    passes.append((ident_bf[:, :], MASK_K[:, s.c, :]))
                            else:
                                p4 = [STACK[:, 4 * (s.g % SETS) + i, :] for i in range(4)]
                                passes = [(p4[0][:, s.c * P:(s.c + 1) * P], p4[1]),
                                          (p4[2][0:96, s.c * P:(s.c + 1) * P], p4[3][0:96, :])]
                            for i, (kk, qq) in enumerate(passes):
                                for half in range(2):
                                    last = nc.tensor.matmul(PS[:, bank + half, :], kk, qq[:, half * HALF:(half + 1) * HALF],
                                                            start=i == 0, stop=i == len(passes) - 1)
                        else:
                            pe.wait_ge(m_spread, s.ms)
                            per = s.a.heads // 2
                            for i in range(2):
                                head = 2 * s.pair + i
                                f, hh = divmod(head, per)
                                half = slice(s.half * HALF, (s.half + 1) * HALF)
                                dst = PS[0:C, bank + i, :]
                                k_hi, k_lo = KBD[:, 0, f, hh, :], KBD[:, 1, f, hh, :]
                                q_hi, q_lo = QK[:, 0, f, half], QK[:, 1, f, half]
                                nc.tensor.matmul(dst, k_hi, q_hi, start=True, stop=False)
                                nc.tensor.matmul(dst, k_lo, q_hi, start=False, stop=False)
                                nc.tensor.matmul(dst, k_hi, q_lo, start=False, stop=False)
                                last = nc.tensor.matmul(dst, OF_HEAD[:, head, :], MS[:, s.half, :],
                                                        start=False, stop=True)
                        last.then_inc(km_filled, 1)
                    elif k == "pv":
                        pe.wait_ge(exp_done, s.units[-1])
                        bufs = [PR[:, (u - 1) % PBUFS, :] for u in s.units]
                        if s.a.own:
                            start, stop = s.c == 0, s.c == TILES - 1
                            if start and s.acc:
                                pe.wait_ge(acc_copied, s.acc)
                            if s.a.dh == 16:
                                for hl in range(2):
                                    for half in range(2):
                                        at = 64 * hl + 32 * half
                                        last = nc.tensor.matmul(
                                            PS[at:at + 32, ACC, :], V16[:, s.c, 2 * s.g + hl, :],
                                            bufs[hl][:, half * HALF:(half + 1) * HALF], start=start, stop=stop)
                            else:
                                for half in range(2):
                                    last = nc.tensor.matmul(
                                        PS[64 * half:64 * half + 64, ACC, :], V64[:, s.c, 64 * s.g:64 * s.g + 64],
                                        bufs[0][:, half * HALF:(half + 1) * HALF], start=start, stop=stop)
                                for half in range(2):
                                    at = 64 * (s.c % 2) + 32 * half
                                    last = nc.tensor.matmul(
                                        PS[at:at + 32, DEN, :], ones[:, 0:32], bufs[0][:, half * HALF:(half + 1) * HALF],
                                        start=s.c < 2, stop=s.c >= TILES - 2)
                        else:
                            if s.acc > 1:
                                pe.wait_ge(acc_copied, s.acc - 1)
                            if s.a.dh == 16:
                                for i in range(4):
                                    last = nc.tensor.matmul(
                                        PS[32 * i:32 * i + 32, ACC, :], V16[0:C, 0, 4 * s.g + i, :],
                                        bufs[i // 2][0:C, i % 2 * HALF:(i % 2 + 1) * HALF], start=True, stop=True)
                            else:
                                for i in range(2):
                                    head = 2 * s.g + i
                                    last = nc.tensor.matmul(
                                        PS[64 * i:64 * i + 64, ACC, :], V64[0:C, 0, 64 * head:64 * head + 64],
                                        bufs[0][0:C, i * HALF:(i + 1) * HALF], start=True, stop=True)
                                for i in range(2):
                                    last = nc.tensor.matmul(
                                        PS[32 * i:32 * i + 32, DEN, :], ones[0:C, 0:32],
                                        bufs[0][0:C, i * HALF:(i + 1) * HALF], start=True, stop=True)
                        last.then_inc(pv_done, 1)
                    elif k == "turn":
                        if s.free[0]:
                            pe.wait_ge(exp_done, s.free[0])
                        if s.free[1]:
                            pe.wait_ge(attended, s.free[1])
                        pe.wait_ge(acc_copied, s.acc)
                        bank = KM + 2 * ((s.slot - 1) % 2)
                        parts = [P] if s.a.dh == 16 else [P, P if s.a.own else 64]
                        for j, rows_ in enumerate(parts):
                            for i in range(4):
                                last = nc.tensor.transpose(PS[:, bank + j, i * P:i * P + rows_],
                                                           ACCS[0:rows_, j, i * P:(i + 1) * P], ident[0:rows_, 0:rows_])
                        last.then_inc(turned, 1)
                nc.tensor.drain().then_inc(ended, 1)
                pe.wait_ge(cleared, b + 1)

        @block.scalar
        def _(act):
            act.wait_ge(vectors_turned, 1)
            nc.scalar.activation(COL[:, :, :].rearrange("p f v -> p (f v)"), PS[:, 0, 0:FH * VECTORS],
                                 ACT.Copy).then_inc(vectors_turned, 1)
            act.wait_ge(vectors_turned, 2)
            with nc.scalar.Fori(0, B) as b:
                for s in steps:
                    k = s.kind
                    if s.reuse is not None:
                        bank = PS[:, s.bank, :]
                        if s.by != "dve":
                            act.wait_ge(job_filled, s.job)
                    if k == "to_features_ctx":
                        nc.scalar.activation(CT[:, :, :].rearrange("p f n -> p (f n)"), bank[:, 0:FH * C],
                                             ACT.Copy).then_inc(act_emptied, 1)
                    elif k == "to_features":
                        dst = HT[:, s.f, s.half * HALF:(s.half + 1) * HALF]
                        if s.scaled is None:
                            nc.scalar.activation(dst, bank, ACT.Copy).then_inc(act_emptied, 1)
                        else:
                            nc.scalar.activation(dst, bank, ACT.Identity, bias=COL[:, s.f, s.scaled + 1:s.scaled + 2],
                                                 scale=COL[:, s.f, s.scaled:s.scaled + 1]).then_inc(act_emptied, 1)
                    elif k == "key_row":
                        nc.scalar.activation(KEY_ROW[:, s.part * HALF:(s.part + 1) * HALF], bank,
                                             ACT.Copy).then_inc(act_emptied, 1)
                    elif k == "project_kq":
                        n = HALF if s.side == "q" or s.a.own else C
                        col = QK_COL + 2 * s.a.number + (s.side == "k")
                        part = 0 if s.side == "q" else 2
                        nc.scalar.activation(QK[:, part, s.f, s.half * HALF:s.half * HALF + n], bank[:, 0:n],
                                             ACT.Relu if s.a.relu else ACT.Identity,
                                             bias=COL[:, s.f, col:col + 1]).then_inc(hi_written, 1)
                    elif k == "hidden":
                        col = FF_COL + s.f // 2
                        nc.scalar.activation(HID[:, s.f, s.half * HALF:(s.half + 1) * HALF], bank, ACT.Relu,
                                             bias=COL[:, s.f % 2, col:col + 1]).then_inc(act_emptied, 1)
                    elif k == "km":
                        if s.pv_before:
                            act.wait_ge(pv_done, s.pv_before)
                        act.wait_ge(km_filled, s.exp)
                        bank = KM + 2 * ((s.slot - 1) % 2)
                        rows_ = P if s.a.own else C
                        bias = 0.0
                        if s.a.keyed:
                            bias = kneg[:, s.c:s.c + 1] if s.a.own else cneg[:, 0:1]
                            act.wait_ge(sums_done, s.sums)
                        nc.scalar.activation(PR[0:rows_, s.buf, :],
                                             PS[0:rows_, bank:bank + 2, :].rearrange("p a n -> p (a n)"),
                                             ACT.Exp, bias=bias, scale=s.a.scale).then_inc(exp_done, 1)
                    elif k == "pv" and s.last:
                        act.wait_ge(pv_done, s.pv)
                        if s.acc > 1:
                            act.wait_ge(turned, s.acc - 1)
                        if s.a.dh == 16:
                            nc.scalar.activation(ACCS[:, 0, :], PS[:, ACC, :], ACT.Copy).then_inc(acc_copied, 1)
                        else:
                            rows_ = P if s.a.own else 64
                            nc.scalar.activation(ACCS[:, 0, :], PS[:, ACC, :], ACT.Copy)
                            nc.scalar.activation(ACCS[0:rows_, 1, :], PS[0:rows_, DEN, :],
                                                 ACT.Copy).then_inc(acc_copied, 1)
                nc.scalar.drain().then_inc(ended, 1)
                act.wait_ge(cleared, b + 1)

        @block.vector
        def _(dve):
            dve.wait_ge(constants, CONSTANTS)
            dve.wait_ge(masks_in, 32)
            nc.vector.tensor_scalar(MASK_Q[:, :, :], RAW[:, 0], -1.0, BIG, ALU.add, ALU.mult)
            nc.vector.tensor_scalar(MASK_K[:, :, :], RAW[:, 1], -1.0, BIG, ALU.add, ALU.mult)
            nc.vector.drain().then_inc(masks_in, 1)
            with nc.vector.Fori(0, B) as b:
                chain = [0]

                def link(ins):
                    chain[0] += 1
                    ins.then_inc(dve_chain, 1)

                def settle():
                    dve.wait_ge(dve_chain, chain[0])

                for s in steps:
                    k = s.kind
                    if s.reuse is not None:
                        bank = PS[:, s.bank, :]
                        if s.by == "dve":
                            dve.wait_ge(job_filled, s.job)
                    if k == "load":
                        dve.wait_ge(loaded, 32)
                        link(nc.vector.tensor_reduce(csum[:, :], CX[:, :], AX.X, ALU.add))
                        settle()
                        link(nc.vector.tensor_scalar(cneg[:, :], csum[:, :], 0.0, NEG, ALU.is_equal, ALU.mult))
                        settle()
                        link(nc.vector.tensor_scalar(cneg_raw[:, :], cneg[:, :], 8.0, None, ALU.mult))
                        settle()
                        for i in range(2):
                            link(nc.vector.tensor_scalar(cdiag[:, i, :], ident[0:C, 0:C], cneg_raw[:, 0:1], None,
                                                         ALU.mult))
                    elif k == "sums":
                        dve.wait_ge(dve_emptied, s.dve)
                        link(nc.vector.tensor_reduce(rowsum[:, :], X[:, :, :], AX.X, ALU.add))
                        settle()
                        link(nc.vector.tensor_scalar(qmask[:, :], rowsum[:, :], 0.0, None, ALU.not_equal))
                        link(nc.vector.tensor_scalar(kneg[:, :], rowsum[:, :], 0.0, NEG, ALU.is_equal, ALU.mult))
                        settle()
                        nc.vector.tensor_scalar(kneg_raw[:, :], kneg[:, :], 8.0, None, ALU.mult).then_inc(sums_done, 1)
                        dve.wait_ge(sums_done, s.sums)
                    elif k == "key_row":
                        if s.part == 1:
                            dve.wait_ge(job_filled, s.job - 1)
                        for i in range(4):
                            t = 4 * s.part + i
                            nc.vector.tensor_scalar(diag[:, i, :], ident[:, :], kneg_raw[:, t:t + 1], None,
                                                    ALU.mult).then_inc(diag_done, 1)
                    elif k == "norm":
                        settle()
                        dve.wait_ge(dve_emptied, s.dve) if s.dve else None
                        for t in range(TILES):
                            link(nc.vector.bn_stats(stats[:, t, :], X[:, t, :]))
                        settle()
                        for t in range(TILES):
                            link(nc.vector.bn_aggr(mv[:, t, :], stats[:, t, :]))
                        settle()
                        if s.eps is None:
                            nc.vector.tensor_scalar(var[:, :], mv[:, :, 1], D / (D - 1.0), None,
                                                    ALU.mult).then_inc(var_ready, 1)
                        else:
                            nc.vector.tensor_scalar(var[:, :], mv[:, :, 1], s.eps, None, ALU.add).then_inc(var_ready, 1)
                        dve.wait_ge(rstd_ready, s.ln)
                        scale = rstd
                        if s.eps is None:
                            link(nc.vector.tensor_scalar(var[:, :], rstd[:, :], 1e-8, None, ALU.add))
                            settle()
                            link(nc.vector.reciprocal(SUM[:, 0:TILES], var[:, :]))
                            settle()
                            scale = SUM
                        if s.into == "features":
                            dve.wait_ge(job_filled, s.job)
                            for t in range(TILES):
                                nc.vector.tensor_scalar(XN[:, t, :], X[:, t, :], mv[:, t, 0:1], scale[:, t:t + 1],
                                                        ALU.subtract, ALU.mult).then_inc(xn_ready, 1)
                        else:
                            gamma = 1 if s.phase in (3, 4, 5, 7) else 2
                            for t in range(TILES):
                                link(nc.vector.scalar_tensor_tensor(
                                    out=XN[:, t, :], in0=X[:, t, :], scalar=mv[:, t, 0:1], in1=r(s, gamma),
                                    op0=ALU.subtract, op1=ALU.mult))
                            settle()
                            for t in range(TILES):
                                nc.vector.scalar_tensor_tensor(
                                    out=X[:, t, :], in0=XN[:, t, :], scalar=scale[:, t:t + 1], in1=r(s, gamma + 1),
                                    op0=ALU.mult, op1=ALU.add).then_inc(x_ready, 1)
                            dve.wait_ge(x_ready, s.x)
                    elif k == "project_kq":
                        dve.wait_ge(hi_written, s.kq)
                        n = HALF if s.side == "q" or s.a.own else C
                        col = QK_COL + 2 * s.a.number + (s.side == "k")
                        part = 0 if s.side == "q" else 2
                        at = slice(s.half * HALF, s.half * HALF + n)
                        if s.a.relu:
                            if s.a.own and s.qm:
                                dve.wait_ge(qm_reduced, s.qm)
                            link(nc.vector.tensor_scalar(TMP[:, 0:n], bank[:, 0:n], COL[:, s.f, col:col + 1], 0.0,
                                                         ALU.add, ALU.max))
                            settle()
                            nc.vector.tensor_tensor(QK[:, part + 1, s.f, at], TMP[:, 0:n],
                                                    QK[:, part, s.f, at].bitcast(F32),
                                                    ALU.subtract).then_inc(dve_emptied, 1)
                            dve.wait_ge(dve_emptied, s.dve)
                        else:
                            nc.vector.scalar_tensor_tensor(
                                out=QK[:, part + 1, s.f, at], in0=bank[:, 0:n], scalar=COL[:, s.f, col:col + 1],
                                in1=QK[:, part, s.f, at].bitcast(F32), op0=ALU.add,
                                op1=ALU.subtract).then_inc(dve_emptied, 1)
                    elif k == "project_v":
                        dve.wait_ge(pads_set, s.pads)
                        n = P if s.a.own else C
                        if s.a.dh == 16:
                            nc.vector.tensor_tensor(
                                V16[0:n, s.t, :, 0:16], bank[0:n, 0:D].rearrange("p (h e) -> p h e", e=16),
                                r(s, 0, n).rearrange("p (h e) -> p h e", e=16), ALU.add).then_inc(dve_emptied, 1)
                        else:
                            if s.a.own and s.qm:
                                dve.wait_ge(qm_reduced, s.qm)
                            link(nc.vector.tensor_tensor(TMP[0:n, 0:D], bank[0:n, 0:D], r(s, 0, n), ALU.add))
                            settle()
                            nc.vector.tensor_scalar(V64[0:n, s.t, :], TMP[0:n, 0:D], 0.0, None,
                                                    ALU.max).then_inc(dve_emptied, 1)
                            dve.wait_ge(dve_emptied, s.dve)
                    elif k == "spread_keys":
                        dve.wait_ge(dve_emptied, s.dve)
                        dve.wait_ge(pads_set, s.pads)
                        per = s.a.heads // 2
                        blocks = block16 if s.a.dh == 16 else block64
                        for i in range(2):
                            for f in range(FH):
                                src = QK[:, 2 + i, f, 0:C].bitcast(F32)
                                link(nc.vector.tensor_tensor(
                                    KBD[:, i, f, 0:per, :], src.rearrange("p (o k) -> p o k", o=1).to_broadcast([P, per, C]),
                                    blocks[:, :].rearrange("p (h o) -> p h o", o=1).to_broadcast([P, per, C]), ALU.mult))
                        nc.vector.tensor_copy(OF_HEAD, of_head[:, :].rearrange("p (h o) -> p h o", o=1)
                                              .to_broadcast([P, 16, C]))
                        nc.vector.drain().then_inc(keys_spread, 1)
                    elif k == "qm":
                        dve.wait_ge(qm_filled, s.qm)
                        if s.a.own:
                            to = M[:, s.g % 2, s.half, s.tile:s.tile + 1]
                            keys = slice(s.half * HALF, (s.half + 1) * HALF)
                            if s.a.masked:
                                lowered = MASK_Q[:, s.tile % TILES, keys]
                            else:
                                lowered = KEY_ROW[:, keys]
                                if s.tile == 0 and s.g == 0:
                                    dve.wait_ge(act_emptied, s.act)
                            if s.qm > 1:
                                dve.wait_ge(qm_reduced, s.qm - 1)
                            nc.vector.tensor_tensor_reduce(DUMP[:, keys], PS[:, s.bank, :], lowered, 1.0, -3e38,
                                                           ALU.add, ALU.max, to).then_inc(qm_reduced, 1)
                        else:
                            if s.a.dh == 16:
                                per = 4
                                at = 8 * s.f + 4 * s.half
                            else:
                                per = 2
                                at = 2 * s.f
                            nc.vector.tensor_reduce(
                                MC[:, s.tile, at:at + per], PS[:, s.bank, 0:per * C].rearrange("p (h k) -> p h k", k=C),
                                AX.X, ALU.max).then_inc(qm_reduced, 1)
                    elif k == "join":
                        cols = 2 * TILES if s.a.dh == 16 else TILES
                        dve.wait_ge(qm_reduced, s.qm)
                        if s.m:
                            dve.wait_ge(m_turned, s.m)
                        nc.vector.tensor_tensor(MJ[:, s.g % 2, 0:cols], M[:, s.g % 2, 0, 0:cols],
                                                M[:, s.g % 2, 1, 0:cols], ALU.max).then_inc(m_joined, 1)
                    elif k == "m":
                        dve.wait_ge(m_turned, s.m)
                        if s.a.own:
                            cols = 2 * TILES if s.a.dh == 16 else TILES
                            if s.placed:
                                dve.wait_ge(m_placed, s.placed)
                            nc.vector.tensor_scalar(MT[0:cols, s.m % 2, :], PS[0:cols, s.bank, 0:P],
                                                    LOWEST if s.a.masked else -3e38, -1.0, ALU.max,
                                                    ALU.mult).then_inc(m_written, 1)
                        else:
                            nc.vector.tensor_scalar(MTC[:, :], PS[:, s.bank, 0:P], -1.0, None,
                                                    ALU.mult).then_inc(m_written, 1)
                            dve.wait_ge(m_written, s.m)
                            nc.vector.tensor_tensor(
                                MS[:, s.half, :].rearrange("p (t n) -> p t n", t=4),
                                MTC[:, :].rearrange("p (o n) -> p o n", o=1).to_broadcast([P, 4, P]),
                                block16[:, 4 * s.half:4 * s.half + 4].rearrange("p (t o) -> p t o", o=1)
                                .to_broadcast([P, 4, P]), ALU.mult).then_inc(m_spread, 1)
                            dve.wait_ge(m_spread, s.ms)
                    elif k == "turn":
                        dve.wait_ge(turned, s.turn)
                        if s.turn > 1:
                            dve.wait_ge(attended, s.turn - 1)
                        bank = KM + 2 * ((s.slot - 1) % 2)
                        if s.a.dh == 16:
                            vals = PS[:, bank, :].rearrange("p (k j e) -> p k j e", k=4, e=32)
                            link(nc.vector.reciprocal(REC[:, :].rearrange("p (k j) -> p k j", k=4), vals[:, :, :, 16]))
                            settle()
                            rec = REC[:, :].rearrange("p (k j o) -> p k j o", k=4, o=1)
                            if s.a.own:
                                for hl in range(2):
                                    head = 2 * s.g + hl
                                    for half in range(2):
                                        j = 2 * hl + half
                                        last = nc.vector.tensor_tensor(
                                            XN[:, 4 * half:4 * half + 4, 16 * head:16 * head + 16], vals[:, :, j, 0:16],
                                            rec[:, :, j, :].to_broadcast([P, 4, 16]), ALU.mult)
                                        if (hl, half) == (1, 1):
                                            last.then_inc(attended, 1)
                            else:
                                nc.vector.tensor_tensor(
                                    XN[:, 4 * s.half:4 * s.half + 4, 64 * s.g:64 * s.g + 64]
                                    .rearrange("p k (j e) -> p k j e", e=16), vals[:, :, :, 0:16],
                                    rec.to_broadcast([P, 4, 4, 16]), ALU.mult).then_inc(attended, 1)
                        else:
                            vals = PS[:, bank, :].rearrange("p (k j e) -> p k j e", k=4, j=2)
                            sums = PS[:, bank + 1, :].rearrange("p (k c j e) -> p k c j e", k=4, c=2, j=2)
                            if s.a.own:
                                link(nc.vector.tensor_reduce(SUM[:, 8:16].rearrange("p (k j) -> p k j", k=4),
                                                             sums[:, :, :, :, 0].rearrange("p k c j -> p k j c"),
                                                             AX.X, ALU.add))
                            else:
                                link(nc.vector.tensor_copy(SUM[:, 8:16].rearrange("p (k j) -> p k j", k=4),
                                                           sums[:, :, 0, :, 0]))
                            settle()
                            link(nc.vector.reciprocal(REC[:, 0:8], SUM[:, 8:16]))
                            settle()
                            rec = REC[:, 0:8].rearrange("p (k j) -> p k j", k=4)
                            to = REC[:, 8:16].rearrange("p (k j) -> p k j", k=4)
                            if s.a.own:
                                q = qmask[:, :].rearrange("p (j k) -> p k j", j=2)
                            else:
                                q = qmask[:, 4 * s.half:4 * s.half + 4].rearrange("p (k o) -> p k o", o=1)\
                                    .to_broadcast([P, 4, 2])
                            link(nc.vector.tensor_tensor(to, rec, q, ALU.mult))
                            settle()
                            for j in range(2):
                                if s.a.own:
                                    dst = XN[:, 4 * j:4 * j + 4, 64 * s.g:64 * s.g + 64]
                                else:
                                    head = 2 * s.g + j
                                    dst = XN[:, 4 * s.half:4 * s.half + 4, 64 * head:64 * head + 64]
                                last = nc.vector.tensor_tensor(
                                    dst, vals[:, :, j, :], to[:, :, j:j + 1].to_broadcast([P, 4, 64]), ALU.mult)
                            last.then_inc(attended, 1)
                    elif k == "end_attention":
                        dve.wait_ge(attended, s.turn)
                    elif k == "add_attended":
                        nc.vector.tensor_tensor(X[:, :, :], X[:, :, :], XN[:, :, :], ALU.add).then_inc(x_ready, 1)
                        dve.wait_ge(x_ready, s.x)
                    elif k in ("add_projected", "add_hidden"):
                        if s.t == 0:
                            dve.wait_ge(x_biased, s.xb)
                        nc.vector.tensor_tensor(X[:, s.t, :], bank[:, 0:D], X[:, s.t, :], ALU.add)\
                            .then_inc(dve_emptied, 1)
                    elif k == "leaky":
                        link(nc.vector.tensor_tensor(TMP[:, 0:D], bank[:, 0:D], r(s, 3), ALU.add))
                        settle()
                        link(nc.vector.scalar_tensor_tensor(out=TMP[:, D:2 * D], in0=TMP[:, 0:D], scalar=0.2,
                                                            in1=TMP[:, 0:D], op0=ALU.mult, op1=ALU.max))
                        settle()
                        nc.vector.tensor_tensor(X[:, s.t, :], TMP[:, D:2 * D], X[:, s.t, :], ALU.add)\
                            .then_inc(dve_emptied, 1)
                    elif k == "phase":
                        wait_weights(dve, s)
                    elif k == "phase_end":
                        nc.vector.drain().then_inc(phase_done, 1)
                nc.vector.drain().then_inc(ended, 1)
                dve.wait_ge(cleared, b + 1)


def kernel(**inputs):
    import numpy as np
    import concourse.bacc as bacc
    from concourse.bass_utils import run_bass_kernel_spmd

    def get(name):
        return np.asarray(inputs[name])

    def matrix(a):
        k = a.shape[0] // P
        return a.reshape(k, P, a.shape[1]).transpose(1, 0, 2).reshape(P, -1)

    l0, l1, l2, l3 = (f"L{i}_xattn_" for i in range(4))
    matrices = [get(l0 + n) for n in ("sa_wq", "sa_wk", "sa_wv", "sa_wo", "ca_wq", "ca_wk", "ca_wv", "ca_wo",
                                      "ff_w1", "ff_w2")]
    for i in range(3):
        matrices += [get(l1 + n)[i] for n in ("Wq", "Wk", "Wv", "Wff")]
    matrices += [get(l2 + n).T for n in ("Wq", "Wk", "Wv", "Wo")]
    matrices += [get(l3 + n) for n in ("Wq", "Wk", "Wv")]
    weights = np.ascontiguousarray(np.concatenate([matrix(m) for m in matrices], axis=1))

    phase_rows = [[get(l0 + "sa_bv"), get(l0 + "sa_bo")], [get(l0 + "ca_bv"), get(l0 + "ca_bo")], [get(l0 + "ff_b2")]]
    phase_rows += [[get(l1 + n)[i] for n in ("bv", "gamma", "beta", "bff")] for i in range(3)]
    phase_rows += [[get(l2 + n) for n in ("bv", "bo", "gamma", "beta")]]
    phase_rows += [[get(l3 + n) for n in ("bv", "ln_gamma", "ln_beta")]]
    rows = np.stack([np.stack(list(p) + [p[0]] * (ROWS - len(p))) for p in phase_rows])

    vectors = [get(l0 + n) for n in ("ln1_g", "ln1_b", "ln2_g", "ln2_b", "ln3_g", "ln3_b")]
    vectors += list(get(l0 + "ff_b1").reshape(FF // D, D))
    vectors += [get(l0 + n) for n in ("sa_bq", "sa_bk", "ca_bq", "ca_bk")]
    vectors += [get(l1 + n)[i] for i in range(3) for n in ("bq", "bk")]
    vectors += [get(l + n) for l in (l2, l3) for n in ("bq", "bk")]
    vectors = np.stack(vectors)

    mask = np.ascontiguousarray(get("mask_1x1xSxS_bk0").reshape(T, T))
    mask, mask_t = (np.ascontiguousarray(a).view(np.int32) for a in (mask, mask.T))
    arrays = {"x": np.ascontiguousarray(get("x")), "context": np.ascontiguousarray(get("ctx_1024")),
              "mask": mask, "mask_t": mask_t,
              "weights": weights, "rows": rows, "vectors": vectors}
    nc = bacc.Bacc("TRN2", target_bir_lowering=False, num_devices=1, dynamic_dma_scratch_size=1024)
    args = [nc.dram_tensor(n, a.shape, mybir.dt.from_np(a.dtype), kind="ExternalInput").ap() for n, a in arrays.items()]
    args.append(nc.dram_tensor("out", (B, T, D), F32, kind="ExternalOutput").ap())
    attention_stack(nc, *args)
    r = run_bass_kernel_spmd(nc, [arrays], core_ids=[0])
    return r.results[0]["out"]
```

```python
from contextlib import ExitStack

import concourse.bass as bass
from concourse import mybir

F32 = mybir.dt.float32
F32R = mybir.dt.float32r
BF16 = mybir.dt.bfloat16
U8 = mybir.dt.uint8
I32 = mybir.dt.int32
ALU = mybir.AluOpType
ACT = mybir.ActivationFunctionType
AX = mybir.AxisListType

P = 128
B, T, D = 4, 1024, 256
C = 77
TILES = T // P
HALF = 512
FH = D // P
FF = 4 * D
BIG = 1e30
LOWEST = -1e29
NEG = -4294967295.0
PAD = 64
RING = [0, 1, 2, 3, 6]
KM, ACC, DEN = 0, 6, 7
QM_RING = {16: [4, 5, 7], 64: [4, 5]}
SETS = 3
LEAD = {16: 5, 64: 4}
PAIR = {16: 2, 64: 1}
PADDED_16 = [0, 2, 8, 10, 1, 3, 5, 7, 9, 11]
STACK_DMAS = {16: 4, 64: 4}
PBUFS = 6


class Attention:
    def __init__(self, number, dh, own, relu, masked, scale):
        self.number, self.dh, self.own, self.relu, self.masked, self.scale = number, dh, own, relu, masked, scale
        self.keyed = relu
        self.heads = D // dh


ATTENTIONS = [Attention(0, 16, True, False, True, 0.25), Attention(1, 16, False, False, False, 0.25),
              Attention(2, 64, False, True, False, 0.125), Attention(3, 64, True, True, False, 0.125),
              Attention(4, 64, True, True, False, 0.125), Attention(5, 16, False, False, False, 1.0 / 16),
              Attention(6, 16, False, False, False, 0.25)]

UNIT = FH * D
PHASE_UNITS = [4, 4, 8, 4, 4, 4, 4, 3]
PHASE_AT = [sum(PHASE_UNITS[:i]) * UNIT for i in range(8)]
ROWS = 4
LN_COL = [0, 2, 4]
FF_COL = 6
QK_COL = 10
NORM_COL = {3: QK_COL + 2 * len(ATTENTIONS)}
NORM_COL.update({p: NORM_COL[3] + 2 * (p - 3) for p in (4, 5, 6)})
VECTORS = NORM_COL[6] + 2


class Counts:
    def __init__(self):
        self.job = self.act = self.dve = self.kq = 0
        self.slot = self.exp = self.turn = 0
        self.qm = self.m = self.placed = 0
        self.rowsums = self.done = self.done_pool = 0
        self.joined = self.keys = 0
        self.pv = self.acc = 0
        self.ln = self.xn = self.xb = 0
        self.bd = self.ms = self.pads = self.sums = 0
        self.stacked = (0,) * SETS
        self.phase = 0


class Step:
    def __init__(self, n, kind, a=None, by=None, bank=0, reuse=None, free=None, first=False, last=False,
                 g=0, c=0, hl=0, half=0, pair=0, head=0, t=0, tile=0, f=0, side="", source="", scaled=None,
                 part=0, row=0, after=0, eps=None, buf=0, units=None):
        self.kind, self.a, self.by, self.bank, self.reuse, self.free = kind, a, by, bank, reuse, free
        self.first, self.last, self.g, self.c, self.hl, self.half, self.pair = first, last, g, c, hl, half, pair
        self.head, self.t, self.tile, self.f, self.side, self.source, self.scaled = head, t, tile, f, side, source, scaled
        self.part, self.row, self.after, self.eps, self.buf, self.units = part, row, after, eps, buf, units
        self.job, self.act, self.dve, self.kq, self.slot, self.exp = n.job, n.act, n.dve, n.kq, n.slot, n.exp
        self.turn, self.qm, self.m, self.placed, self.pv, self.acc = n.turn, n.qm, n.m, n.placed, n.pv, n.acc
        self.ln, self.xn, self.xb, self.bd, self.ms = n.ln, n.xn, n.xb, n.bd, n.ms
        self.pads, self.sums, self.stacked, self.phase = n.pads, n.sums, n.stacked, n.phase
        self.joined, self.keys = n.joined, n.keys
        self.rowsums, self.done, self.done_pool = n.rowsums, n.done, n.done_pool
        self.pv_before = 0


def schedule():
    steps = []
    n = Counts()
    jobs = {0: (0, 0)}
    slots = {}

    def put(kind, **place):
        steps.append(Step(n, kind, **place))

    def job(kind, by, **kw):
        n.job += 1
        n.act += by == "act"
        n.dve += by in ("dve", "both")
        n.kq += by == "both"
        jobs[n.job] = (n.act, n.dve)
        put(kind, by=by, bank=RING[(n.job - 1) % len(RING)], reuse=jobs.get(n.job - len(RING), (0, 0)), **kw)

    def turn_in(source, half, scaled=None, after=0):
        for f in range(FH):
            job("to_features", "act", source=source, scaled=scaled, half=half, f=f, after=after)

    def stats(half, eps):
        n.ln += 1
        rstd_at[half] = n.ln
        put("stats", half=half, eps=eps)

    def normalise(half, eps):
        n.xn += 4
        put("normalise", half=half, eps=eps, after=rstd_at[half])
        xn_at[half] = n.xn

    def scale_x(half, side, row):
        if side == "pool":
            n.done_pool += 1
        else:
            n.done += 1
        put("scale_x", half=half, side=side, row=row)

    def add_tiles(kind, eps=None):
        for t in range(TILES):
            job(kind, "dve", t=t)
            dve_at[t] = n.dve
            if kind != "add_projected" and n.phase < 5:
                n.rowsums += 1
                put("rowsum", t=t, after=n.dve)
            if eps is not None and t == 4:
                stats(0, eps)
            if eps is not None and t == 6:
                normalise(0, eps)
        if eps is not None:
            stats(1, eps)
            normalise(1, eps)

    rstd_at, xn_at, dve_at = {}, {}, {}

    def take_slot():
        n.slot += 1
        return slots.get(n.slot - 2, (0, 0))

    def attend(a):
        put("begin_attention", a=a)
        if not a.relu and a.number < 6:
            n.xb += 1
            put("bias_x", row=1)
        if a.own:
            self_attention(a)
        elif a.dh == 16:
            cross_attention_16(a)
        else:
            cross_attention_64(a)
        put("end_attention", a=a)

    def km(a, **kw):
        free = take_slot()
        n.exp += 1
        slots[n.slot] = (n.exp, n.turn)
        put("km", a=a, free=free, buf=(n.exp - 1) % PBUFS, **kw)

    def pv(a, last, units, **kw):
        n.pv += 1
        n.acc += last
        for u in units:
            pv_of_exp[u] = n.pv
        put("pv", a=a, last=last, units=units, **kw)

    def turn(a, **kw):
        if a.own or a.dh == 64:
            free = take_slot()
            n.turn += 1
            slots[n.slot] = (n.exp, n.turn)
            put("turn", a=a, free=(*free, 0), bank=KM + 2 * ((n.slot - 1) % 2), **kw)
        else:
            used, place = take_qm_bank(a)
            n.turn += 1
            used.append((0, 0, n.turn))
            put("turn", a=a, **place, **kw)

    def take_qm_bank(a):
        if a not in qm_banks:
            qm_banks.clear()
            qm_banks[a] = []
        used, ring = qm_banks[a], QM_RING[a.dh]
        return used, dict(bank=ring[len(used) % len(ring)],
                          free=used[-len(ring)] if len(used) >= len(ring) else (0, 0, 0))

    def qm(a, **kw):
        used, place = take_qm_bank(a)
        n.qm += 1
        used.append((n.qm, 0, 0))
        put("qm", a=a, **place, **kw)

    def m(a, **kw):
        used, place = take_qm_bank(a)
        n.m += 1
        used.append((0, n.m, 0))
        put("m", a=a, **place, **kw)
        if a.own:
            n.placed += 16 * PAIR[a.dh]

    qm_banks = {}

    def stack(a, g):
        dmas = 16 * PAIR[a.dh] * (STACK_DMAS[a.dh] if a.own else 2)
        n.stacked = tuple(c + dmas * (i == g % SETS) for i, c in enumerate(n.stacked))
        put("stack", a=a, g=g)

    pv_of_exp = {}

    def kq(a, side, f, half):
        job("project_kq", "both", a=a, side=side, f=f, half=half)

    def v(a, t):
        job("project_v", "dve", a=a, t=t)

    def self_attention(a):
        per = PAIR[a.dh]
        groups = a.heads // per
        units = TILES * per
        for half in range(2):
            kq(a, "k", 0, half)
        for half in range(2):
            kq(a, "q", 0, half)
        for g in range(SETS):
            if g * per * a.dh < P:
                stack(a, g)
        exp0 = n.exp
        maxima = iter([(g, i) for g in range(groups) for i in range(units)])

        def take_maxima(tiles=1):
            for _ in range(tiles):
                g, i = next(maxima, (0, None))
                if i is not None:
                    for half in range(2):
                        qm(a, g=g, tile=i, half=half)
                    if i == units - 1:
                        n.joined += 1
                        put("join", a=a, g=g)

        rest = [("v", t) for t in range(TILES)] + [(s, h) for s in "kq" for h in range(2)]
        start = TILES if per == 2 else TILES // 2
        for i, (what, x) in enumerate(rest):
            if what == "v":
                v(a, x)
            else:
                kq(a, what, 1, x)
            if a.keyed and i in (1, 3):
                job("key_row", "act", part=i // 2)
            if i >= start:
                take_maxima()
        for g in range(SETS):
            if g * per * a.dh >= P:
                stack(a, g)
        take_maxima(units - (len(rest) - start))
        m(a, g=0)
        take_maxima(LEAD[a.dh])
        for g in range(groups):
            for i in range(units):
                c, hl = divmod(i, per)
                km(a, g=g, c=c, hl=hl, head=g * per + hl, first=i == 0)
                take_maxima()
                if hl == per - 1:
                    if c == 0 and g > 0:
                        pv(a, True, [exp0 + g * units - k for k in range(per)][::-1], g=g - 1, c=TILES - 1)
                    if c >= 1:
                        pv(a, False, [exp0 + g * units + (c - 1) * per + k + 1 for k in range(per)], g=g, c=c - 1)
                    if c == 2 and g > 0:
                        turn(a, g=g - 1)
                if i == units - LEAD[a.dh] + 1 and g + 1 < groups:
                    m(a, g=g + 1)
                if i == units - 1 and g + SETS < groups:
                    stack(a, g + SETS)
        pv(a, True, [n.exp - k for k in range(per)][::-1], g=groups - 1, c=TILES - 1)
        turn(a, g=groups - 1)

    def prepare_context(a):
        for f in range(FH):
            kq(a, "k", f, 0)
        v(a, 0)
        n.bd += 1
        put("spread_keys", a=a)
        if a.dh == 16:
            n.keys += 16 * 2 * a.heads
            put("stack_keys", a=a)

    def cross_attention_16(a):
        groups = a.heads // 2
        for f in range(FH):
            for half in range(2):
                kq(a, "q", f, half)
            if f == 0:
                for g in range(SETS):
                    stack(a, g)

        def rows(g):
            n.stacked = tuple(c + 32 * (i == g % SETS) for i, c in enumerate(n.stacked))
            put("rows", a=a, g=g)

        for t in range(TILES):
            for half in range(2):
                qm(a, tile=t, f=0, half=half)
        m(a, f=0)
        for g in range(SETS):
            rows(g)
        later = iter([(t, half) for t in range(TILES) for half in range(2)])
        for _ in range(4):
            t, half = next(later)
            qm(a, tile=t, f=1, half=half)
        for g in range(groups):
            for hl in range(2):
                km(a, g=g, c=0, hl=hl, head=2 * g + hl, first=hl == 0)
                for _ in range(4):
                    t, half = next(later, (0, None))
                    if half is not None:
                        qm(a, tile=t, f=1, half=half)
            if g + SETS < groups:
                stack(a, g + SETS)
                if g + SETS != 4:
                    rows(g + SETS)
            if g > 0:
                pv(a, True, [n.exp - 3, n.exp - 2], g=g - 1, c=0)
            if g > 1:
                turn(a, g=g - 2)
            if g == 1:
                m(a, f=1)
                rows(4)
        turn(a, g=groups - 2)
        pv(a, True, [n.exp - 1, n.exp], g=groups - 1, c=0)
        turn(a, g=groups - 1)

    def cross_attention_64(a):
        for f in range(FH):
            kq(a, "q", f, 0)
        group = 2
        for t in range(4):
            for f in range(FH):
                qm(a, tile=t, f=f)
        for f in range(FH):
            kq(a, "q", f, 1)
        n.ms += 1
        m(a, half=0)
        later = iter([(t, f) for t in range(4, 8) for f in range(FH)])
        each = 4
        pending = None
        for half in range(2):
            for g in range(a.heads // group):
                km(a, half=half, pair=g, first=half + g == 0)
                units = [n.exp]
                if half == 0:
                    for _ in range(each):
                        t, f = next(later)
                        qm(a, tile=t, f=f)
                if pending:
                    turn(a, **pending)
                    if half == 1 and g == 0:
                        stats(0, None)
                pv(a, True, units, half=half, g=g)
                pending = dict(half=half, g=g)
            if half == 0:
                n.ms += 1
                m(a, half=1)
        turn(a, **pending)

    def phase(number):
        n.phase = number
        put("phase")

    def next_phase():
        put("phase_end")

    def prepare(number, a):
        n.pads += 1
        put("pads", a=a)
        if not a.own:
            here = n.phase
            phase(number)
            prepare_context(a)
            n.phase = here

    put("load")
    job("to_features_ctx", "act")
    phase(0)
    for half in range(2):
        stats(half, 1e-5)
    prepare(0, ATTENTIONS[0])
    for half in range(2):
        normalise(half, 1e-5)
    put("context_mask")
    for p in range(2):
        for half in range(2):
            turn_in("xn", half, LN_COL[p], xn_at[half])
        attend(ATTENTIONS[p])
        if p == 0:
            prepare(1, ATTENTIONS[1])
        for half in range(2):
            turn_in("attended", half)
        add_tiles("add_projected", eps=1e-5)
        next_phase()
        phase(p + 1)
    for half in range(2):
        turn_in("xn", half, LN_COL[2], xn_at[half])
    n.xb += 1
    put("bias_x", row=0)
    for f in range(FF // P):
        for half in range(2):
            job("hidden", "act", f=f, half=half)
    add_tiles("add_hidden")
    next_phase()
    prepare(3, ATTENTIONS[2])
    for p in range(3, 6):
        phase(p)
        for half in range(2):
            turn_in("x", half, after=dve_at[4 * half + 3])
        n.sums += 1
        put("sums")
        attend(ATTENTIONS[p - 1])
        for half in range(1 if p == 3 else 0, 2):
            stats(half, None)
        for half in range(2):
            normalise(half, None)
        for half in range(2):
            turn_in("xn", half, NORM_COL[p], xn_at[half])
        scale_x(0, "dve", row=1)
        scale_x(1, "pool", row=1)
        prepare(p + 1, ATTENTIONS[p])
        add_tiles("leaky")
        next_phase()
    phase(6)
    for half in range(2):
        turn_in("x", half, after=dve_at[4 * half + 3])
    attend(ATTENTIONS[5])
    prepare(7, ATTENTIONS[6])
    for half in range(2):
        turn_in("attended", half)
    add_tiles("add_projected", eps=1e-5)
    for half in range(2):
        turn_in("xn", half, NORM_COL[6], xn_at[half])
    scale_x(0, "dve", row=2)
    scale_x(1, "pool", row=2)
    next_phase()
    put("next_weights", part=0)
    phase(7)
    attend(ATTENTIONS[6])
    put("next_weights", part=1)
    for half in range(2):
        stats(half, 1e-6)
    for half in range(2):
        normalise(half, 1e-6)
        scale_x(half, "dve", row=1)
        put("store", half=half)
    next_phase()
    for s in steps:
        if s.kind == "km":
            s.pv_before = pv_of_exp.get(s.exp - PBUFS, 0)
    return steps


def attention_stack(nc, x, ctx_in, mask, mask_t, weights, rows, vectors, out):
    steps = schedule()
    stacks_at = {(s.a, s.g): s.stacked[s.g % SETS] for s in steps if s.kind == "stack"}
    rows_at = {(s.a, s.g): s.stacked[s.g % SETS] for s in steps if s.kind == "rows"}
    joined_at = {(s.a, s.g): s.joined for s in steps if s.kind == "join"}
    ctx = ExitStack()
    with ctx:
        def sb(name, shape, dt=F32):
            return ctx.enter_context(nc.sbuf_tensor(name, shape, dt))

        def sem(name):
            cleared_each_batch.append(ctx.enter_context(nc.semaphore(name)))
            return cleared_each_batch[-1]

        cleared_each_batch = []
        X = sb("X", [P, TILES, D])
        XN = sb("XN", [P, TILES, D])
        HT = sb("HT", [P, FH, T])
        QK = sb("QK", [P, 4, FH, T], F32R)
        VP = sb("VP", [P, 4096 + PBUFS * T])
        STACK = sb("STACK", [P, 4 * SETS, T], F32R)
        MASK_Q = sb("MASK_Q", [P, TILES, T], BF16)
        MASK_K = sb("MASK_K", [P, TILES, T], BF16)
        W = [sb("W_even", [P, 8 * UNIT]), sb("W_odd", [P, 4 * UNIT])]
        R = [sb("R_even", [P, ROWS, D]), sb("R_odd", [P, ROWS, D])]
        KEY_ROW = sb("KEY_ROW", [P, T], BF16)
        CT = sb("CT", [P, FH, C])
        COL = sb("COL", [P, FH, VECTORS])
        ACCS = sb("ACCS", [P, 2, HALF])
        CX = ACCS[0:C, 0, 0:D]
        TMP = sb("TMP", [P, HALF])
        VEC = TMP[0:VECTORS, 0:D]
        ident = sb("ident", [P, P])
        ident_bf = sb("ident_bf", [P, P], BF16)
        ones = sb("ones", [P, P])
        block16 = sb("block16", [P, 8])
        block64 = sb("block64", [P, 2])
        of_head = sb("of_head", [P, 16])
        half_power = sb("half_power", [P, 2, TILES])
        stats = sb("stats", [P, TILES, 6])
        mv = sb("mv", [P, TILES, 2])
        var = sb("var", [P, TILES])
        rstd = sb("rstd", [P, TILES])
        M = sb("M", [P, 2, 2, 16])
        MJ = sb("MJ", [P, 2, 16])
        MC = sb("MC", [P, P])
        MT = sb("MT", [P, 2, P], F32R)
        MTC = TMP[:, 0:P]
        REC = sb("REC", [P, 16])
        SUM = sb("SUM", [P, 16])
        rowsum = sb("rowsum", [P, TILES])
        qmask = sb("qmask", [P, TILES])
        kneg = sb("kneg", [P, TILES])
        kneg_raw = sb("kneg_raw", [P, TILES])
        csum = sb("csum", [C, 1])
        cneg = sb("cneg", [C, 1])
        cneg_raw = sb("cneg_raw", [C, 1])
        cdiag = sb("cdiag", [C, 2, C], F32R)
        diag = TMP[:, :].rearrange("p (t n) -> p t n", t=4)
        PS = ctx.enter_context(nc.psum_tensor("PS", [P, 8, HALF], F32))

        V = VP[:, 0:4096]
        V16 = V.rearrange("p (c h e) -> p c h e", h=16, e=32)
        V64 = VP[:, 0:TILES * D].rearrange("p (c n) -> p c n", c=TILES)
        PR = VP[:, 4096:4096 + PBUFS * T].rearrange("p (u n) -> p u n", u=PBUFS)
        HID = VP[:, 0:FF // P * T].rearrange("p (f n) -> p f n", f=FF // P)
        WORDS = VP[:, 0:2 * TILES * T // 4].bitcast(I32).rearrange("p (a t n) -> p a t n", a=2, t=TILES)
        RAW = VP[:, 0:2 * TILES * T // 4].bitcast(U8).rearrange("p (a t n) -> p a t n", a=2, t=TILES)
        def spread(a, i, f):
            if a.dh == 16:
                return STACK[:, 4 + 2 * f, 0:8 * C].rearrange("p (h k) -> p h k", h=8)
            return KBD[:, i, f, 0:2, :]

        def stacked_keys(head):
            return STACK[:, 2 * (head // 8), head % 8 * C:(head % 8 + 1) * C]

        KBD = STACK[:, 0:4, :].rearrange("p a n -> p (a n)")[:, 0:4 * 8 * C].rearrange(
            "p (a f h k) -> p a f h k", a=2, f=FH, h=8)
        MS = STACK[:, 4, :].rearrange("p (a n) -> p a n", a=2)
        OF_HEAD = STACK[:, 5, 0:4 * C].rearrange("p (h k) -> p h k", h=4)
        DUMP = TMP[:, :].bitcast(BF16)

        x_loaded = [sem("x_loaded_0"), sem("x_loaded_1")]
        ctx_loaded = sem("ctx_loaded")
        next_in = sem("next_in")
        weights_in = [sem("weights_even"), sem("weights_odd")]
        job_filled = sem("job_filled")
        act_emptied = sem("act_emptied")
        dve_emptied = sem("dve_emptied")
        hi_written = sem("hi_written")
        xn_ready = sem("xn_ready")
        rowsummed = sem("rowsummed")
        x_scaled = sem("x_scaled")
        x_scaled_pool = sem("x_scaled_pool")
        var_ready = sem("var_ready")
        rstd_ready = sem("rstd_ready")
        x_biased = sem("x_biased")
        pads_set = sem("pads_set")
        stacked = [sem(f"stacked_{i}") for i in range(SETS)]
        qm_filled = sem("qm_filled")
        qm_reduced = sem("qm_reduced")
        m_joined = sem("m_joined")
        m_turned = sem("m_turned")
        m_written = sem("m_written")
        m_placed = sem("m_placed")
        km_filled = sem("km_filled")
        exp_done = sem("exp_done")
        pv_done = sem("pv_done")
        acc_filled = sem("acc_filled")
        acc_copied = sem("acc_copied")
        turned = sem("turned")
        attended = sem("attended")
        keys_spread = sem("keys_spread")
        keys_stacked = sem("keys_stacked")
        m_spread = sem("m_spread")
        sums_done = sem("sums_done")
        diag_done = sem("diag_done")
        phase_done = sem("phase_done")
        dve_chain = sem("dve_chain")
        pool_chain = sem("pool_chain")
        stored = sem("stored")
        constants = ctx.enter_context(nc.semaphore("constants"))
        first_weights = ctx.enter_context(nc.semaphore("first_weights"))
        set_up = ctx.enter_context(nc.semaphore("set_up"))
        masks_in = ctx.enter_context(nc.semaphore("masks_in"))
        vectors_in = ctx.enter_context(nc.semaphore("vectors_in"))
        vectors_turned = ctx.enter_context(nc.semaphore("vectors_turned"))
        ended = ctx.enter_context(nc.semaphore("ended"))
        cleared = ctx.enter_context(nc.semaphore("cleared"))
        CONSTANTS = 1

        block = ctx.enter_context(nc.Block())

        def w(s, unit, k, lo, hi):
            base = unit * UNIT + k * D
            return W[s.phase % 2][:, base + lo:base + hi]

        def copy_of(s, group):
            return group % 2 if s.a.dh == 16 else 0

        def wait_weights(engine, s):
            if s.phase > 1:
                engine.wait_ge(weights_in[s.phase % 2], 32 * (s.phase // 2))

        def r(s, row, parts=P):
            return R[s.phase % 2][0:parts, row, :]

        @block.sync
        def _(sp):
            sp.dma_start(VEC[:, :], vectors).then_inc(vectors_in, 16)
            sp.dma_start(WORDS[:, 0], mask.rearrange("(t p) n -> p t n", p=P)).then_inc(masks_in, 16)
            sp.dma_start(WORDS[:, 1], mask_t.rearrange("(t p) n -> p t n", p=P)).then_inc(masks_in, 16)

            def load_matrices(phase, semaphore):
                lo, size = PHASE_AT[phase], PHASE_UNITS[phase] * UNIT
                sp.dma_start(W[phase % 2][:, 0:size], weights[:, lo:lo + size]).then_inc(semaphore, 16)

            def load_rows(phase, semaphore):
                sp.dma_start(R[phase % 2][:, :, :], rows[phase:phase + 1].to_broadcast([P, ROWS, D]))\
                    .then_inc(semaphore, 16)

            for phase in range(2):
                load_matrices(phase, first_weights)
                load_rows(phase, first_weights)
            with nc.sync.Fori(0, B) as b:
                for s in steps:
                    if s.kind == "phase_end" and s.phase + 2 < 8:
                        sp.wait_ge(phase_done, s.phase + 1)
                        load_matrices(s.phase + 2, weights_in[s.phase % 2])
                        load_rows(s.phase + 2, weights_in[s.phase % 2])
                    elif s.kind == "next_weights" and s.part == 0:
                        sp.wait_ge(phase_done, s.phase + 1)
                        sp.wait_ge(x_scaled_pool, s.done_pool)
                        load_matrices(0, next_in)
                        load_rows(0, next_in)
                    elif s.kind == "next_weights":
                        sp.wait_ge(job_filled, s.job)
                        load_matrices(1, next_in)
                    elif s.kind == "load":
                        for half in range(2):
                            sp.dma_start(X[:, 4 * half:4 * half + 4, :],
                                         x[b].rearrange("(t p) d -> p t d", p=P)[:, 4 * half:4 * half + 4, :])\
                                .then_inc(x_loaded[half], 16)
                        sp.dma_start(CX[:, :], ctx_in[b]).then_inc(ctx_loaded, 16)
                    elif s.kind == "stack":
                        a, g = s.a, s.g
                        per = PAIR[a.dh]
                        f = g * per * a.dh // P
                        sp.wait_ge(dve_emptied, s.dve)
                        if g < SETS:
                            sp.wait_ge(pads_set, s.pads)
                        else:
                            sp.wait_ge(km_filled, s.exp)
                        for hl in range(per):
                            head = g * per + hl
                            lo = head * a.dh % P
                            q_parts, k_parts = (QK[lo:lo + a.dh, i:i + 2, f, :].bitcast(F32) for i in (0, 2))
                            if a.dh == 16:
                                k_plane, q_plane = (
                                    STACK[:, 2 * (g % SETS * 2 + hl) + i, :].bitcast(F32) for i in range(2))
                                for i in range(2):
                                    if a.own:
                                        sp.dma_start(k_plane[32 * i:32 * i + 32, :], k_parts)\
                                            .then_inc(stacked[g % SETS], 16)
                                    sp.dma_start(q_plane[32 * i:32 * i + 32, :],
                                                 q_parts[:, i:i + 1, :].to_broadcast([16, 2, T]))\
                                        .then_inc(stacked[g % SETS], 16)
                            else:
                                planes = [STACK[:, 4 * (g % SETS) + i, :].bitcast(F32) for i in range(4)]
                                for to, part in ((planes[0], k_parts),
                                                 (planes[1], q_parts[:, 0:1, :].to_broadcast([64, 2, T])),
                                                 (planes[2][0:64, :], k_parts[:, 0, :]),
                                                 (planes[3][0:64, :], q_parts[:, 1, :])):
                                    sp.dma_start(to, part).then_inc(stacked[g % SETS], 16)
                    elif s.kind == "stack_keys":
                        sp.wait_ge(dve_emptied, s.dve)
                        sp.wait_ge(pads_set, s.pads)
                        for head in range(s.a.heads):
                            lo, f = 16 * (head % 8), head // 8
                            for i in range(2):
                                sp.dma_start(stacked_keys(head)[32 * i:32 * i + 32, :].bitcast(F32),
                                             QK[lo:lo + 16, 2:4, f, 0:C].bitcast(F32)).then_inc(keys_stacked, 16)
                    elif s.kind == "rows":
                        sp.wait_ge(m_written, s.m)
                        at = 2 * s.g % 8 * TILES
                        plane = 4 * (s.g % SETS) + 1
                        for hl in range(2):
                            sp.dma_start(STACK[96:97, plane + 2 * hl, :].bitcast(F32),
                                         MT[at + TILES * hl:at + TILES * (hl + 1), s.g // 4, :].bitcast(F32))\
                                .then_inc(stacked[s.g % SETS], 16)
                    elif s.kind == "m" and s.a.own:
                        sp.wait_ge(m_written, s.m)
                        plane = 4 * (s.g % SETS)
                        for hl in range(PAIR[s.a.dh]):
                            if s.a.dh == 16:
                                row = STACK[96:97, plane + 2 * hl + 1, :]
                            else:
                                row = STACK[64:65, plane + 3, :]
                            sp.dma_start(row.bitcast(F32), MT[hl * TILES:(hl + 1) * TILES, s.m % 2, :].bitcast(F32))\
                                .then_inc(m_placed, 16)
                    elif s.kind == "store":
                        sp.wait_ge(x_scaled, s.done)
                        sp.dma_start(out[b].rearrange("(t p) d -> p t d", p=P)[:, 4 * s.half:4 * s.half + 4, :],
                                     X[:, 4 * s.half:4 * s.half + 4, :]).then_inc(stored, 16)
                load_rows(1, next_in)
                sp.wait_ge(next_in, 64)
                sp.wait_ge(stored, 32)
                sp.wait_ge(ended, 4 * b + 4)
                sp.sem_inc(stored, 1)
                for semaphore in cleared_each_batch:
                    sp.sem_clear(semaphore)
                sp.sem_inc(cleared, 1)

        @block.gpsimd
        def _(pool):
            made = [0]

            def then(ins):
                made[0] += 1
                ins.then_inc(set_up, 1)
                pool.wait_ge(set_up, made[0])

            then(nc.gpsimd.memset(ident[:, :], 0.0))
            then(nc.gpsimd.affine_select(out=ident[:, :], in_=ident[:, :], compare_op=ALU.not_equal, fill=1.0,
                                         base=0, pattern=[[-1, P]], channel_multiplier=1))
            then(nc.gpsimd.tensor_copy(ident_bf[:, :], ident[:, :]))
            then(nc.gpsimd.memset(ones[:, :], 1.0))
            then(nc.gpsimd.memset(half_power[:, 0, :], -0.5))
            then(nc.gpsimd.memset(half_power[:, 1, :], 0.5))
            then(nc.gpsimd.memset(MC[:, :], 0.0))
            for tile, width in ((block16, 16), (block64, 64)):
                cols = P // width
                then(nc.gpsimd.memset(tile[:, :], 1.0))
                then(nc.gpsimd.affine_select(out=tile[:, :], in_=tile[:, :], compare_op=ALU.is_ge, fill=0.0,
                                             base=0, pattern=[[-width, cols]], channel_multiplier=1))
                then(nc.gpsimd.affine_select(out=tile[:, :], in_=tile[:, :], compare_op=ALU.is_ge, fill=0.0,
                                             base=width - 1, pattern=[[width, cols]], channel_multiplier=-1))
            then(nc.gpsimd.memset(of_head[:, :], 0.0))
            for t in range(8):
                then(nc.gpsimd.affine_select(out=of_head[:, :], in_=of_head[:, :], compare_op=ALU.not_equal,
                                             fill=1.0, base=-16 * t, pattern=[[-1, 16]], channel_multiplier=1))
            nc.gpsimd.drain().then_inc(constants, 1)

            pool.wait_ge(masks_in, 33)
            pool.wait_ge(first_weights, 64)
            for plane in PADDED_16:
                then(nc.gpsimd.memset(STACK[PAD:PAD + (32 if plane % 2 else 33), plane, :].bitcast(F32),
                                      0.0 if plane % 2 else 1.0))
            with nc.gpsimd.Fori(0, B) as b:
                links = [0]

                def link(ins):
                    links[0] += 1
                    ins.then_inc(pool_chain, 1)
                    pool.wait_ge(pool_chain, links[0])

                def pads_16():
                    for plane in PADDED_16:
                        if plane % 2:
                            link(nc.gpsimd.memset(STACK[PAD:96, plane, :].bitcast(F32), 0.0))
                        else:
                            link(nc.gpsimd.memset(STACK[PAD:97, plane, :].bitcast(F32), 1.0))

                for s in steps:
                    if s.kind == "stats":
                        pool.wait_ge(var_ready, s.ln)
                        tiles = slice(4 * s.half, 4 * s.half + 4)
                        nc.gpsimd.tensor_tensor(rstd[:, tiles], var[:, tiles],
                                                half_power[:, 1 if s.eps is None else 0, tiles],
                                                ALU.pow).then_inc(rstd_ready, 1)
                        pool.wait_ge(rstd_ready, s.ln)
                    elif s.kind == "scale_x" and s.side == "pool":
                        pool.wait_ge(xn_ready, s.xn)
                        tiles = slice(4 * s.half, 4 * s.half + 4)
                        gamma, beta = (R[s.phase % 2][:, row:row + 1, :].to_broadcast([P, 4, D])
                                       for row in (s.row, s.row + 1))
                        link(nc.gpsimd.tensor_tensor(X[:, tiles, :], XN[:, tiles, :], gamma, ALU.mult))
                        nc.gpsimd.tensor_tensor(X[:, tiles, :], X[:, tiles, :], beta, ALU.add)\
                            .then_inc(x_scaled_pool, 1)
                        pool.wait_ge(x_scaled_pool, s.done_pool)
                    elif s.kind == "bias_x":
                        pool.wait_ge(xn_ready, s.xn)
                        pool.wait_ge(job_filled, s.job)
                        wait_weights(pool, s)
                        nc.gpsimd.tensor_tensor(
                            X[:, :, :], X[:, :, :], R[s.phase % 2][:, s.row:s.row + 1, :].to_broadcast([P, TILES, D]),
                            ALU.add).then_inc(x_biased, 1)
                        pool.wait_ge(x_biased, s.xb)
                    elif s.kind == "pads":
                        if s.turn:
                            pool.wait_ge(attended, s.turn)
                        pool.wait_ge(job_filled, s.job)
                        if s.a.number == 0:
                            for plane in (4, 6):
                                link(nc.gpsimd.memset(STACK[PAD:97, plane, :].bitcast(F32), 1.0))
                            link(nc.gpsimd.memset(V16[:, :, :, 16:32], 1.0))
                        elif s.a.number == 3:
                            for slot in range(SETS):
                                link(nc.gpsimd.memset(STACK[64:96, 4 * slot + 2, :].bitcast(F32), 1.0))
                                link(nc.gpsimd.memset(STACK[64:96, 4 * slot + 3, :].bitcast(F32), 0.0))
                        elif s.a.number == 5:
                            link(nc.gpsimd.memset(V16[:, 0:1, :, 16:32], 1.0))
                            pads_16()
                        nc.gpsimd.drain().then_inc(pads_set, 1)
                    elif s.kind == "spread_keys":
                        pool.wait_ge(dve_emptied, s.dve)
                        per = s.a.heads // 2
                        blocks = block16 if s.a.dh == 16 else block64
                        for i in range(1 if s.a.dh == 16 else 2):
                            for f in range(FH):
                                src = QK[:, 2 + i, f, 0:C].bitcast(F32)
                                link(nc.gpsimd.tensor_tensor(
                                    spread(s.a, i, f), src.rearrange("p (o k) -> p o k", o=1).to_broadcast([P, per, C]),
                                    blocks[:, 0:per].rearrange("p (h o) -> p h o", o=1).to_broadcast([P, per, C]),
                                    ALU.mult))
                        if s.a.dh == 64:
                            link(nc.gpsimd.tensor_copy(OF_HEAD, of_head[:, 0:4].rearrange("p (h o) -> p h o", o=1)
                                                       .to_broadcast([P, 4, C])))
                        nc.gpsimd.drain().then_inc(keys_spread, 1)
                nc.gpsimd.drain().then_inc(ended, 1)
                pool.wait_ge(cleared, b + 1)

        @block.tensor
        def _(pe):
            pe.wait_ge(constants, CONSTANTS)
            pe.wait_ge(vectors_in, 16)
            for f in range(FH):
                last = nc.tensor.transpose(PS[:, 0, f * VECTORS:(f + 1) * VECTORS], VEC[:, f * P:(f + 1) * P],
                                           ident[0:VECTORS, 0:VECTORS])
            last.then_inc(vectors_turned, 1)
            pe.wait_ge(vectors_turned, 2)
            pe.wait_ge(masks_in, 33)
            pe.wait_ge(first_weights, 64)
            with nc.tensor.Fori(0, B) as b:
                for s in steps:
                    k = s.kind
                    if s.reuse is not None:
                        if s.reuse[0]:
                            pe.wait_ge(act_emptied, s.reuse[0])
                        if s.reuse[1]:
                            pe.wait_ge(dve_emptied, s.reuse[1])
                        bank = PS[:, s.bank, :]
                    if k == "phase":
                        wait_weights(pe, s)
                    elif k == "begin_attention":
                        pe.wait_ge(act_emptied, s.act)
                        if s.dve:
                            pe.wait_ge(dve_emptied, s.dve)
                    elif k == "end_attention":
                        pe.wait_ge(attended, s.turn)
                    elif k == "to_features_ctx":
                        pe.wait_ge(ctx_loaded, 16)
                        for f in range(FH):
                            last = nc.tensor.transpose(bank[:, f * C:(f + 1) * C], CX[:, f * P:(f + 1) * P],
                                                       ident[0:C, 0:C])
                        last.then_inc(job_filled, 1)
                    elif k == "to_features":
                        source = X if s.source == "x" else XN
                        for i in range(4):
                            t = 4 * s.half + i
                            if s.source == "xn":
                                pe.wait_ge(xn_ready, s.after - 3 + i)
                            elif i == 0 and s.source == "x":
                                pe.wait_ge(dve_emptied, s.after)
                            last = nc.tensor.transpose(bank[:, i * P:(i + 1) * P], source[:, t, s.f * P:(s.f + 1) * P],
                                                       ident[:, :])
                        last.then_inc(job_filled, 1)
                    elif k == "key_row":
                        pe.wait_ge(diag_done, 4 * (2 * (s.phase - 4) + s.part + 1))
                        for i in range(4):
                            last = nc.tensor.matmul(bank[:, i * P:(i + 1) * P], ones[:, :], diag[:, i, :],
                                                    start=True, stop=True)
                        last.then_inc(job_filled, 1)
                    elif k == "project_kq":
                        own = s.side == "q" or s.a.own
                        n = HALF if own else C
                        for i in range(FH):
                            src = HT[:, i, s.half * HALF:(s.half + 1) * HALF] if own else CT[:, i, :]
                            last = nc.tensor.matmul(bank[:, 0:n], w(s, 0 if s.side == "q" else 1, i, s.f * P, s.f * P + P),
                                                    src, start=i == 0, stop=i == FH - 1)
                        last.then_inc(job_filled, 1)
                    elif k == "project_v":
                        n = P if s.a.own else C
                        for i in range(FH):
                            src = HT[:, i, s.t * P:(s.t + 1) * P] if s.a.own else CT[:, i, :]
                            last = nc.tensor.matmul(bank[0:n, 0:D], src, w(s, 2, i, 0, D), start=i == 0, stop=i == FH - 1)
                        last.then_inc(job_filled, 1)
                    elif k in ("add_projected", "leaky"):
                        if s.t == 0:
                            pe.wait_ge(act_emptied, s.act)
                        for i in range(FH):
                            last = nc.tensor.matmul(bank[:, 0:D], HT[:, i, s.t * P:(s.t + 1) * P], w(s, 3, i, 0, D),
                                                    start=i == 0, stop=i == FH - 1)
                        last.then_inc(job_filled, 1)
                    elif k == "hidden":
                        if s.f == 0 and s.half == 0:
                            pe.wait_ge(act_emptied, s.act - 1)
                        for i in range(FH):
                            last = nc.tensor.matmul(bank, W[0][:, i * FF + s.f * P:i * FF + (s.f + 1) * P],
                                                    HT[:, i, s.half * HALF:(s.half + 1) * HALF],
                                                    start=i == 0, stop=i == FH - 1)
                        last.then_inc(job_filled, 1)
                    elif k == "add_hidden":
                        if s.t == 0:
                            pe.wait_ge(act_emptied, s.act)
                        for i in range(FF // P):
                            base = 4 * UNIT + i * D
                            last = nc.tensor.matmul(bank[:, 0:D], HID[:, i, s.t * P:(s.t + 1) * P],
                                                    W[0][:, base:base + D], start=i == 0, stop=i == FF // P - 1)
                        last.then_inc(job_filled, 1)
                    elif k == "qm":
                        if s.free[0]:
                            pe.wait_ge(qm_reduced, s.free[0])
                        if s.free[1]:
                            pe.wait_ge(m_written, s.free[1])
                        if s.free[2]:
                            pe.wait_ge(attended, s.free[2])
                        if s.a.own:
                            if s.tile == 0 and s.half == 0:
                                pe.wait_ge(stacked[s.g % SETS], stacks_at[s.a, s.g])
                                if s.g == 0:
                                    pe.wait_ge(pads_set, s.pads)
                            if s.a.dh == 16:
                                hl, t = divmod(s.tile, TILES)
                                base = 2 * (s.g % SETS * 2 + hl)
                                kk, qq = STACK[0:96, base, :], STACK[0:96, base + 1, t * P:(t + 1) * P]
                            else:
                                kk = STACK[:, 4 * (s.g % SETS), :]
                                qq = STACK[:, 4 * (s.g % SETS) + 1, s.tile * P:(s.tile + 1) * P]
                            last = nc.tensor.matmul(PS[:, s.bank, :], qq, kk[:, s.half * HALF:(s.half + 1) * HALF],
                                                    start=True, stop=True)
                        else:
                            if s.tile == 0:
                                pe.wait_ge(keys_spread, s.bd)
                            if s.tile % 4 == 0:
                                pe.wait_ge(dve_emptied, s.dve)
                            qq = QK[:, 0, s.f, s.tile * P:(s.tile + 1) * P]
                            if s.a.dh == 16:
                                last = nc.tensor.matmul(
                                    PS[:, s.bank, 0:4 * C], qq,
                                    spread(s.a, 0, s.f)[:, 4 * s.half:4 * s.half + 4, :].rearrange("p h k -> p (h k)"),
                                    start=True, stop=True)
                            else:
                                nc.tensor.matmul(PS[:, s.bank, 0:2 * C], qq,
                                                 KBD[:, 0, s.f, 0:2, :].rearrange("p h k -> p (h k)"),
                                                 start=True, stop=False)
                                last = nc.tensor.matmul(PS[:, s.bank, 0:2 * C], ones[0:C, :].bitcast(F32R),
                                                        cdiag[:, :, :].rearrange("p h k -> p (h k)"),
                                                        start=False, stop=True)
                        last.then_inc(qm_filled, 1)
                    elif k == "m":
                        if s.free[0]:
                            pe.wait_ge(qm_reduced, s.free[0])
                        if s.free[1]:
                            pe.wait_ge(m_written, s.free[1])
                        if s.free[2]:
                            pe.wait_ge(attended, s.free[2])
                        if s.a.own:
                            pe.wait_ge(m_joined, joined_at[s.a, s.g])
                            cols = 2 * TILES if s.a.dh == 16 else TILES
                            last = nc.tensor.transpose(PS[0:cols, s.bank, 0:P], MJ[:, s.g % 2, 0:cols], ident[:, :])
                        elif s.a.dh == 16:
                            pe.wait_ge(qm_reduced, s.qm)
                            last = nc.tensor.transpose(PS[0:64, s.bank, 0:P], MC[:, 64 * s.f:64 * s.f + 64], ident[:, :])
                        else:
                            pe.wait_ge(qm_reduced, s.qm)
                            last = nc.tensor.transpose(PS[:, s.bank, 0:P], MC[:, :],
                                                       ident[:, :])
                        last.then_inc(m_turned, 1)
                    elif k == "km":
                        if s.free[0]:
                            pe.wait_ge(exp_done, s.free[0])
                        if s.free[1]:
                            pe.wait_ge(attended, s.free[1])
                        if s.first:
                            pe.wait_ge(pads_set, s.pads)
                            pe.wait_ge(act_emptied, s.act)
                            pe.wait_ge(dve_emptied, s.dve)
                        bank = KM + 2 * ((s.slot - 1) % 2)
                        if s.a.dh == 16 and not s.a.own:
                            if s.first:
                                pe.wait_ge(stacked[s.g % SETS], rows_at[s.a, s.g])
                                pe.wait_ge(keys_stacked, s.keys)
                            for half in range(2):
                                last = nc.tensor.matmul(
                                    PS[0:C, bank + half, :], stacked_keys(s.head)[0:97, :],
                                    STACK[0:97, 2 * (s.g % SETS * 2 + s.hl) + 1, half * HALF:(half + 1) * HALF],
                                    start=True, stop=True)
                        elif s.a.own:
                            if s.first:
                                pe.wait_ge(m_placed, s.placed)
                                if s.a.dh == 64 and s.g == 0:
                                    pe.wait_ge(pads_set, s.pads)
                            if s.a.dh == 16:
                                base = 2 * (s.g % SETS * 2 + s.hl)
                                passes = [(STACK[0:97, base, s.c * P:(s.c + 1) * P], STACK[0:97, base + 1, :])]
                                if s.a.masked:
                                    passes.append((ident_bf[:, :], MASK_K[:, s.c, :]))
                            else:
                                p4 = [STACK[:, 4 * (s.g % SETS) + i, :] for i in range(4)]
                                passes = [(p4[0][:, s.c * P:(s.c + 1) * P], p4[1]),
                                          (p4[2][0:96, s.c * P:(s.c + 1) * P], p4[3][0:96, :])]
                            for i, (kk, qq) in enumerate(passes):
                                for half in range(2):
                                    last = nc.tensor.matmul(PS[:, bank + half, :], kk, qq[:, half * HALF:(half + 1) * HALF],
                                                            start=i == 0, stop=i == len(passes) - 1)
                        else:
                            pe.wait_ge(m_spread, s.ms)
                            per = s.a.heads // 2
                            for i in range(2):
                                head = 2 * s.pair + i
                                f, hh = divmod(head, per)
                                half = slice(s.half * HALF, (s.half + 1) * HALF)
                                dst = PS[0:C, bank + i, :]
                                k_hi, k_lo = KBD[:, 0, f, hh, :], KBD[:, 1, f, hh, :]
                                q_hi, q_lo = QK[:, 0, f, half], QK[:, 1, f, half]
                                nc.tensor.matmul(dst, k_hi, q_hi, start=True, stop=False)
                                nc.tensor.matmul(dst, k_lo, q_hi, start=False, stop=False)
                                nc.tensor.matmul(dst, k_hi, q_lo, start=False, stop=False)
                                last = nc.tensor.matmul(dst, OF_HEAD[:, head, :], MS[:, s.half, :],
                                                        start=False, stop=True)
                        last.then_inc(km_filled, 1)
                    elif k == "pv":
                        pe.wait_ge(exp_done, s.units[-1])
                        bufs = [PR[:, (u - 1) % PBUFS, :] for u in s.units]
                        if not s.a.own and s.acc > 1:
                            pe.wait_ge(acc_copied, s.acc - 1)
                        if s.a.own:
                            start, stop = s.c == 0, s.c == TILES - 1
                            if start and s.acc:
                                pe.wait_ge(acc_copied, s.acc)
                            if s.a.dh == 16:
                                for hl in range(2):
                                    for half in range(2):
                                        at = 64 * hl + 32 * half
                                        last = nc.tensor.matmul(
                                            PS[at:at + 32, ACC, :], V16[:, s.c, 2 * s.g + hl, :],
                                            bufs[hl][:, half * HALF:(half + 1) * HALF], start=start, stop=stop)
                            else:
                                for half in range(2):
                                    last = nc.tensor.matmul(
                                        PS[64 * half:64 * half + 64, ACC, :], V64[:, s.c, 64 * s.g:64 * s.g + 64],
                                        bufs[0][:, half * HALF:(half + 1) * HALF], start=start, stop=stop)
                                for half in range(2):
                                    at = 64 * (s.c % 2) + 32 * half
                                    last = nc.tensor.matmul(
                                        PS[at:at + 32, DEN, :], ones[:, 0:32], bufs[0][:, half * HALF:(half + 1) * HALF],
                                        start=s.c < 2, stop=s.c >= TILES - 2)
                        elif s.a.dh == 16:
                            for i in range(4):
                                last = nc.tensor.matmul(
                                    PS[32 * i:32 * i + 32, ACC, :], V16[0:C, 0, 2 * s.g + i // 2, :],
                                    bufs[i // 2][0:C, i % 2 * HALF:(i % 2 + 1) * HALF], start=True, stop=True)
                        else:
                            for i in range(2):
                                head = 2 * s.g + i
                                last = nc.tensor.matmul(
                                    PS[64 * i:64 * i + 64, ACC, :], V64[0:C, 0, 64 * head:64 * head + 64],
                                    bufs[0][0:C, i * HALF:(i + 1) * HALF], start=True, stop=True)
                            for i in range(2):
                                last = nc.tensor.matmul(
                                    PS[32 * i:32 * i + 32, DEN, :], ones[0:C, 0:32],
                                    bufs[0][0:C, i * HALF:(i + 1) * HALF], start=True, stop=True)
                        last.then_inc(pv_done, 1)
                    elif k == "turn":
                        if s.a.own or s.a.dh == 64:
                            if s.free[0]:
                                pe.wait_ge(exp_done, s.free[0])
                            if s.free[1]:
                                pe.wait_ge(attended, s.free[1])
                        else:
                            if s.free[0]:
                                pe.wait_ge(qm_reduced, s.free[0])
                            if s.free[1]:
                                pe.wait_ge(m_written, s.free[1])
                            if s.free[2]:
                                pe.wait_ge(attended, s.free[2])
                        pe.wait_ge(acc_copied, s.turn)
                        bank = s.bank
                        parts = [P] if s.a.dh == 16 else [P, P if s.a.own else 64]
                        for j, rows_ in enumerate(parts):
                            for i in range(4):
                                last = nc.tensor.transpose(PS[:, bank + j, i * P:i * P + rows_],
                                                           ACCS[0:rows_, copy_of(s, s.turn) + j, i * P:(i + 1) * P], ident[0:rows_, 0:rows_])
                        last.then_inc(turned, 1)
                nc.tensor.drain().then_inc(ended, 1)
                pe.wait_ge(cleared, b + 1)

        @block.scalar
        def _(act):
            act.wait_ge(vectors_turned, 1)
            nc.scalar.activation(COL[:, :, :].rearrange("p f v -> p (f v)"), PS[:, 0, 0:FH * VECTORS],
                                 ACT.Copy).then_inc(vectors_turned, 1)
            act.wait_ge(vectors_turned, 2)
            with nc.scalar.Fori(0, B) as b:
                for s in steps:
                    k = s.kind
                    if s.reuse is not None:
                        bank = PS[:, s.bank, :]
                        if s.by != "dve":
                            act.wait_ge(job_filled, s.job)
                    if k == "to_features_ctx":
                        nc.scalar.activation(CT[:, :, :].rearrange("p f n -> p (f n)"), bank[:, 0:FH * C],
                                             ACT.Copy).then_inc(act_emptied, 1)
                    elif k == "to_features":
                        dst = HT[:, s.f, s.half * HALF:(s.half + 1) * HALF]
                        if s.scaled is None:
                            nc.scalar.activation(dst, bank, ACT.Copy).then_inc(act_emptied, 1)
                        else:
                            nc.scalar.activation(dst, bank, ACT.Identity, bias=COL[:, s.f, s.scaled + 1:s.scaled + 2],
                                                 scale=COL[:, s.f, s.scaled:s.scaled + 1]).then_inc(act_emptied, 1)
                    elif k == "key_row":
                        nc.scalar.activation(KEY_ROW[:, s.part * HALF:(s.part + 1) * HALF], bank,
                                             ACT.Copy).then_inc(act_emptied, 1)
                    elif k == "project_kq":
                        n = HALF if s.side == "q" or s.a.own else C
                        col = QK_COL + 2 * s.a.number + (s.side == "k")
                        part = 0 if s.side == "q" else 2
                        nc.scalar.activation(QK[:, part, s.f, s.half * HALF:s.half * HALF + n], bank[:, 0:n],
                                             ACT.Relu if s.a.relu else ACT.Identity,
                                             bias=COL[:, s.f, col:col + 1]).then_inc(hi_written, 1)
                    elif k == "rowsum":
                        act.wait_ge(dve_emptied, s.after)
                        if s.t > 1:
                            act.wait_ge(rowsummed, s.rowsums - 2)
                        nc.scalar.activation(ACCS[:, s.t % 2, 0:D], X[:, s.t, :], ACT.Copy,
                                             accum_out=rowsum[:, s.t:s.t + 1]).then_inc(rowsummed, 1)
                    elif k == "hidden":
                        col = FF_COL + s.f // 2
                        nc.scalar.activation(HID[:, s.f, s.half * HALF:(s.half + 1) * HALF], bank, ACT.Relu,
                                             bias=COL[:, s.f % 2, col:col + 1]).then_inc(act_emptied, 1)
                    elif k == "km":
                        if s.pv_before:
                            act.wait_ge(pv_done, s.pv_before)
                        act.wait_ge(km_filled, s.exp)
                        bank = KM + 2 * ((s.slot - 1) % 2)
                        rows_ = P if s.a.own else C
                        bias = 0.0
                        if s.a.keyed:
                            bias = kneg[:, s.c:s.c + 1] if s.a.own else cneg[:, 0:1]
                            act.wait_ge(sums_done, s.sums)
                        nc.scalar.activation(PR[0:rows_, s.buf, :],
                                             PS[0:rows_, bank:bank + 2, :].rearrange("p a n -> p (a n)"),
                                             ACT.Exp, bias=bias, scale=s.a.scale).then_inc(exp_done, 1)
                    elif k == "pv" and s.last:
                        act.wait_ge(pv_done, s.pv)
                        back = 2 if s.a.dh == 16 else 1
                        if s.acc > back:
                            act.wait_ge(turned, s.acc - back)
                        if s.a.dh == 16:
                            nc.scalar.activation(ACCS[:, copy_of(s, s.acc), :], PS[:, ACC, :], ACT.Copy).then_inc(acc_copied, 1)
                        else:
                            rows_ = P if s.a.own else 64
                            nc.scalar.activation(ACCS[:, 0, :], PS[:, ACC, :], ACT.Copy)
                            nc.scalar.activation(ACCS[0:rows_, 1, :], PS[0:rows_, DEN, :],
                                                 ACT.Copy).then_inc(acc_copied, 1)
                nc.scalar.drain().then_inc(ended, 1)
                act.wait_ge(cleared, b + 1)

        @block.vector
        def _(dve):
            dve.wait_ge(constants, CONSTANTS)
            dve.wait_ge(masks_in, 32)
            nc.vector.tensor_scalar(MASK_Q[:, :, :], RAW[:, 0], -1.0, BIG, ALU.add, ALU.mult)
            nc.vector.tensor_scalar(MASK_K[:, :, :], RAW[:, 1], -1.0, BIG, ALU.add, ALU.mult)
            nc.vector.drain().then_inc(masks_in, 1)
            dve.wait_ge(first_weights, 64)
            with nc.vector.Fori(0, B) as b:
                chain = [0]

                def link(ins):
                    chain[0] += 1
                    ins.then_inc(dve_chain, 1)

                def settle():
                    dve.wait_ge(dve_chain, chain[0])

                for s in steps:
                    k = s.kind
                    if s.reuse is not None:
                        bank = PS[:, s.bank, :]
                        if s.by == "dve":
                            dve.wait_ge(job_filled, s.job)
                    if k == "context_mask":
                        dve.wait_ge(ctx_loaded, 16)
                        link(nc.vector.tensor_reduce(csum[:, :], CX[:, :], AX.X, ALU.add))
                        settle()
                        link(nc.vector.tensor_scalar(cneg[:, :], csum[:, :], 0.0, NEG, ALU.is_equal, ALU.mult))
                        settle()
                        link(nc.vector.tensor_scalar(cneg_raw[:, :], cneg[:, :], 8.0, None, ALU.mult))
                        settle()
                        for i in range(2):
                            link(nc.vector.tensor_scalar(cdiag[:, i, :], ident[0:C, 0:C], cneg_raw[:, 0:1], None,
                                                         ALU.mult))
                    elif k == "sums":
                        dve.wait_ge(rowsummed, s.rowsums)
                        link(nc.vector.tensor_scalar(qmask[:, :], rowsum[:, :], 0.0, None, ALU.not_equal))
                        link(nc.vector.tensor_scalar(kneg[:, :], rowsum[:, :], 0.0, NEG, ALU.is_equal, ALU.mult))
                        settle()
                        nc.vector.tensor_scalar(kneg_raw[:, :], kneg[:, :], 8.0, None, ALU.mult).then_inc(sums_done, 1)
                        dve.wait_ge(sums_done, s.sums)
                    elif k == "key_row":
                        if s.part == 1:
                            dve.wait_ge(job_filled, s.job - 1)
                        for i in range(4):
                            t = 4 * s.part + i
                            nc.vector.tensor_scalar(diag[:, i, :], ident[:, :], kneg_raw[:, t:t + 1], None,
                                                    ALU.mult).then_inc(diag_done, 1)
                    elif k == "stats":
                        settle()
                        if s.xn == 0:
                            dve.wait_ge(x_loaded[s.half], 16)
                        if s.dve:
                            dve.wait_ge(dve_emptied, s.dve)
                        tiles = range(4 * s.half, 4 * s.half + 4)
                        for t in tiles:
                            link(nc.vector.bn_stats(stats[:, t, :], X[:, t, :]))
                        settle()
                        for t in tiles:
                            link(nc.vector.bn_aggr(mv[:, t, :], stats[:, t, :]))
                        settle()
                        tiles = slice(4 * s.half, 4 * s.half + 4)
                        if s.eps is None:
                            nc.vector.tensor_scalar(var[:, tiles], mv[:, tiles, 1], D / (D - 1.0), None,
                                                    ALU.mult).then_inc(var_ready, 1)
                        else:
                            nc.vector.tensor_scalar(var[:, tiles], mv[:, tiles, 1], s.eps, None,
                                                    ALU.add).then_inc(var_ready, 1)
                    elif k == "normalise":
                        dve.wait_ge(rstd_ready, s.after)
                        tiles = slice(4 * s.half, 4 * s.half + 4)
                        scale = rstd
                        if s.eps is None:
                            link(nc.vector.tensor_scalar(SUM[:, tiles], rstd[:, tiles], 1e-8, None, ALU.add))
                            settle()
                            link(nc.vector.reciprocal(REC[:, tiles], SUM[:, tiles]))
                            settle()
                            scale = REC
                        dve.wait_ge(job_filled, s.job)
                        for t in range(4 * s.half, 4 * s.half + 4):
                            nc.vector.tensor_scalar(XN[:, t, :], X[:, t, :], mv[:, t, 0:1], scale[:, t:t + 1],
                                                    ALU.subtract, ALU.mult).then_inc(xn_ready, 1)
                    elif k == "scale_x" and s.side == "dve":
                        dve.wait_ge(xn_ready, s.xn)
                        tiles = slice(4 * s.half, 4 * s.half + 4)
                        gamma, beta = (R[s.phase % 2][:, row:row + 1, :].to_broadcast([P, 4, D])
                                       for row in (s.row, s.row + 1))
                        link(nc.vector.tensor_tensor(X[:, tiles, :], XN[:, tiles, :], gamma, ALU.mult))
                        settle()
                        nc.vector.tensor_tensor(X[:, tiles, :], X[:, tiles, :], beta, ALU.add).then_inc(x_scaled, 1)
                    elif k == "project_kq":
                        dve.wait_ge(hi_written, s.kq)
                        n = HALF if s.side == "q" or s.a.own else C
                        col = QK_COL + 2 * s.a.number + (s.side == "k")
                        part = 0 if s.side == "q" else 2
                        at = slice(s.half * HALF, s.half * HALF + n)
                        if s.a.relu:
                            if s.a.own and s.qm:
                                dve.wait_ge(qm_reduced, s.qm)
                            link(nc.vector.tensor_scalar(TMP[:, 0:n], bank[:, 0:n], COL[:, s.f, col:col + 1], 0.0,
                                                         ALU.add, ALU.max))
                            settle()
                            nc.vector.tensor_tensor(QK[:, part + 1, s.f, at], TMP[:, 0:n],
                                                    QK[:, part, s.f, at].bitcast(F32),
                                                    ALU.subtract).then_inc(dve_emptied, 1)
                            dve.wait_ge(dve_emptied, s.dve)
                        else:
                            nc.vector.scalar_tensor_tensor(
                                out=QK[:, part + 1, s.f, at], in0=bank[:, 0:n], scalar=COL[:, s.f, col:col + 1],
                                in1=QK[:, part, s.f, at].bitcast(F32), op0=ALU.add,
                                op1=ALU.subtract).then_inc(dve_emptied, 1)
                    elif k == "project_v":
                        n = P if s.a.own else C
                        if s.a.dh == 16:
                            nc.vector.tensor_tensor(
                                V16[0:n, s.t, :, 0:16], bank[0:n, 0:D].rearrange("p (h e) -> p h e", e=16),
                                r(s, 0, n).rearrange("p (h e) -> p h e", e=16), ALU.add).then_inc(dve_emptied, 1)
                        else:
                            if s.a.own and s.qm:
                                dve.wait_ge(qm_reduced, s.qm)
                            link(nc.vector.tensor_tensor(TMP[0:n, 0:D], bank[0:n, 0:D], r(s, 0, n), ALU.add))
                            settle()
                            nc.vector.tensor_scalar(V64[0:n, s.t, :], TMP[0:n, 0:D], 0.0, None,
                                                    ALU.max).then_inc(dve_emptied, 1)
                            dve.wait_ge(dve_emptied, s.dve)
                    elif k == "qm":
                        dve.wait_ge(qm_filled, s.qm)
                        if s.a.own:
                            to = M[:, s.g % 2, s.half, s.tile:s.tile + 1]
                            keys = slice(s.half * HALF, (s.half + 1) * HALF)
                            if s.a.masked:
                                lowered = MASK_Q[:, s.tile % TILES, keys]
                            else:
                                lowered = KEY_ROW[:, keys]
                                if s.tile == 0 and s.g == 0:
                                    dve.wait_ge(act_emptied, s.act)
                            if s.qm > 2:
                                dve.wait_ge(qm_reduced, s.qm - 2)
                            nc.vector.tensor_tensor_reduce(DUMP[:, keys], PS[:, s.bank, :], lowered, 1.0, -3e38,
                                                           ALU.add, ALU.max, to).then_inc(qm_reduced, 1)
                        else:
                            if s.a.dh == 16:
                                per = 4
                                at = 8 * s.f + 4 * s.half
                                to = MC[:, :].rearrange("p (h t) -> p h t", t=TILES)[:, at:at + per, s.tile]
                            else:
                                per = 2
                                to = MC[:, 16 * s.tile + 2 * s.f:16 * s.tile + 2 * s.f + 2]
                            nc.vector.tensor_reduce(
                                to, PS[:, s.bank, 0:per * C].rearrange("p (h k) -> p h k", k=C),
                                AX.X, ALU.max).then_inc(qm_reduced, 1)
                    elif k == "join":
                        cols = 2 * TILES if s.a.dh == 16 else TILES
                        dve.wait_ge(qm_reduced, s.qm)
                        if s.m:
                            dve.wait_ge(m_turned, s.m)
                        nc.vector.tensor_tensor(MJ[:, s.g % 2, 0:cols], M[:, s.g % 2, 0, 0:cols],
                                                M[:, s.g % 2, 1, 0:cols], ALU.max).then_inc(m_joined, 1)
                    elif k == "m":
                        dve.wait_ge(m_turned, s.m)
                        if s.a.own:
                            cols = 2 * TILES if s.a.dh == 16 else TILES
                            if s.placed:
                                dve.wait_ge(m_placed, s.placed)
                            nc.vector.tensor_scalar(MT[0:cols, s.m % 2, :], PS[0:cols, s.bank, 0:P],
                                                    LOWEST if s.a.masked else -3e38, -1.0, ALU.max,
                                                    ALU.mult).then_inc(m_written, 1)
                        elif s.a.dh == 16:
                            nc.vector.tensor_scalar(MT[0:64, s.f, :], PS[0:64, s.bank, 0:P], -1.0, None,
                                                    ALU.mult).then_inc(m_written, 1)
                        else:
                            nc.vector.tensor_scalar(MTC[:, :], PS[:, s.bank, 0:P], -1.0, None,
                                                    ALU.mult).then_inc(m_written, 1)
                            dve.wait_ge(m_written, s.m)
                            nc.vector.tensor_tensor(
                                MS[:, s.half, :].rearrange("p (t n) -> p t n", t=4),
                                MTC[:, :].rearrange("p (o n) -> p o n", o=1).to_broadcast([P, 4, P]),
                                block16[:, 4 * s.half:4 * s.half + 4].rearrange("p (t o) -> p t o", o=1)
                                .to_broadcast([P, 4, P]), ALU.mult).then_inc(m_spread, 1)
                            dve.wait_ge(m_spread, s.ms)
                    elif k == "turn":
                        adds = s.a.relu or s.a.number == 6
                        if s.done_pool:
                            dve.wait_ge(x_scaled_pool, s.done_pool)
                        dve.wait_ge(turned, s.turn)
                        if s.turn > 1:
                            dve.wait_ge(attended, s.turn - 1)
                        bank = s.bank
                        if s.a.dh == 16:
                            vals = PS[:, bank, :].rearrange("p (k j e) -> p k j e", k=4, e=32)
                            link(nc.vector.reciprocal(REC[:, :].rearrange("p (k j) -> p k j", k=4), vals[:, :, :, 16]))
                            settle()
                            rec = REC[:, :].rearrange("p (k j o) -> p k j o", k=4, o=1)
                            for hl in range(2):
                                head = 2 * s.g + hl
                                for half in range(2):
                                    j = 2 * hl + half
                                    last = nc.vector.tensor_tensor(
                                        XN[:, 4 * half:4 * half + 4, 16 * head:16 * head + 16], vals[:, :, j, 0:16],
                                        rec[:, :, j, :].to_broadcast([P, 4, 16]), ALU.mult)
                            last.then_inc(attended, 1)
                            tiles, cols = slice(0, TILES), slice(32 * s.g, 32 * s.g + 32)
                        else:
                            vals = PS[:, bank, :].rearrange("p (k j e) -> p k j e", k=4, j=2)
                            sums = PS[:, bank + 1, :].rearrange("p (k c j e) -> p k c j e", k=4, c=2, j=2)
                            if s.a.own:
                                link(nc.vector.tensor_reduce(SUM[:, 8:16].rearrange("p (k j) -> p k j", k=4),
                                                             sums[:, :, :, :, 0].rearrange("p k c j -> p k j c"),
                                                             AX.X, ALU.add))
                            else:
                                link(nc.vector.tensor_copy(SUM[:, 8:16].rearrange("p (k j) -> p k j", k=4),
                                                           sums[:, :, 0, :, 0]))
                            settle()
                            link(nc.vector.reciprocal(REC[:, 0:8], SUM[:, 8:16]))
                            settle()
                            rec = REC[:, 0:8].rearrange("p (k j) -> p k j", k=4)
                            to = REC[:, 8:16].rearrange("p (k j) -> p k j", k=4)
                            if s.a.own:
                                q = qmask[:, :].rearrange("p (j k) -> p k j", j=2)
                            else:
                                q = qmask[:, 4 * s.half:4 * s.half + 4].rearrange("p (k o) -> p k o", o=1)\
                                    .to_broadcast([P, 4, 2])
                            link(nc.vector.tensor_tensor(to, rec, q, ALU.mult))
                            settle()
                            for j in range(2):
                                if s.a.own:
                                    dst = XN[:, 4 * j:4 * j + 4, 64 * s.g:64 * s.g + 64]
                                else:
                                    head = 2 * s.g + j
                                    dst = XN[:, 4 * s.half:4 * s.half + 4, 64 * head:64 * head + 64]
                                last = nc.vector.tensor_tensor(
                                    dst, vals[:, :, j, :], to[:, :, j:j + 1].to_broadcast([P, 4, 64]), ALU.mult)
                            last.then_inc(attended, 1)
                            if s.a.own:
                                tiles, cols = slice(0, TILES), slice(64 * s.g, 64 * s.g + 64)
                            else:
                                tiles, cols = slice(4 * s.half, 4 * s.half + 4), slice(128 * s.g, 128 * s.g + 128)
                        if adds:
                            dve.wait_ge(attended, s.turn)
                            link(nc.vector.tensor_tensor(X[:, tiles, cols], X[:, tiles, cols], XN[:, tiles, cols],
                                                         ALU.add))
                    elif k == "end_attention":
                        dve.wait_ge(attended, s.turn)
                    elif k in ("add_projected", "add_hidden"):
                        if s.t == 0:
                            dve.wait_ge(x_biased, s.xb)
                        nc.vector.tensor_tensor(X[:, s.t, :], bank[:, 0:D], X[:, s.t, :], ALU.add)\
                            .then_inc(dve_emptied, 1)
                    elif k == "leaky":
                        if s.t == 0:
                            dve.wait_ge(x_scaled, s.done)
                        if s.t == 4:
                            dve.wait_ge(x_scaled_pool, s.done_pool)
                        link(nc.vector.tensor_tensor(TMP[:, 0:D], bank[:, 0:D], r(s, 3), ALU.add))
                        settle()
                        link(nc.vector.scalar_tensor_tensor(out=TMP[:, D:2 * D], in0=TMP[:, 0:D], scalar=0.2,
                                                            in1=TMP[:, 0:D], op0=ALU.mult, op1=ALU.max))
                        settle()
                        nc.vector.tensor_tensor(X[:, s.t, :], TMP[:, D:2 * D], X[:, s.t, :], ALU.add)\
                            .then_inc(dve_emptied, 1)
                    elif k == "phase":
                        wait_weights(dve, s)
                    elif k == "phase_end":
                        nc.vector.drain().then_inc(phase_done, 1)
                nc.vector.drain().then_inc(ended, 1)
                dve.wait_ge(cleared, b + 1)


def kernel(**inputs):
    import numpy as np
    import concourse.bacc as bacc
    from concourse.bass_utils import run_bass_kernel_spmd

    def get(name):
        return np.asarray(inputs[name])

    def matrix(a):
        k = a.shape[0] // P
        return a.reshape(k, P, a.shape[1]).transpose(1, 0, 2).reshape(P, -1)

    l0, l1, l2, l3 = (f"L{i}_xattn_" for i in range(4))
    matrices = [get(l0 + n) for n in ("sa_wq", "sa_wk", "sa_wv", "sa_wo", "ca_wq", "ca_wk", "ca_wv", "ca_wo",
                                      "ff_w1", "ff_w2")]
    for i in range(3):
        matrices += [get(l1 + n)[i] for n in ("Wq", "Wk", "Wv", "Wff")]
    matrices += [get(l2 + n).T for n in ("Wq", "Wk", "Wv", "Wo")]
    matrices += [get(l3 + n) for n in ("Wq", "Wk", "Wv")]
    weights = np.ascontiguousarray(np.concatenate([matrix(m) for m in matrices], axis=1))

    phase_rows = [[get(l0 + "sa_bv"), get(l0 + "sa_bo")], [get(l0 + "ca_bv"), get(l0 + "ca_bo")], [get(l0 + "ff_b2")]]
    phase_rows += [[get(l1 + n)[i] for n in ("bv", "gamma", "beta", "bff")] for i in range(3)]
    phase_rows += [[get(l2 + n) for n in ("bv", "bo", "gamma", "beta")]]
    phase_rows += [[get(l3 + n) for n in ("bv", "ln_gamma", "ln_beta")]]
    rows = np.stack([np.stack(list(p) + [p[0]] * (ROWS - len(p))) for p in phase_rows])

    vectors = [get(l0 + n) for n in ("ln1_g", "ln1_b", "ln2_g", "ln2_b", "ln3_g", "ln3_b")]
    vectors += list(get(l0 + "ff_b1").reshape(FF // D, D))
    vectors += [get(l0 + n) for n in ("sa_bq", "sa_bk", "ca_bq", "ca_bk")]
    vectors += [get(l1 + n)[i] for i in range(3) for n in ("bq", "bk")]
    vectors += [get(l + n) for l in (l2, l3) for n in ("bq", "bk")]
    vectors += [get(l1 + n)[i] for i in range(3) for n in ("gamma", "beta")]
    vectors += [get(l2 + n) for n in ("gamma", "beta")]
    vectors = np.stack(vectors)

    mask = np.ascontiguousarray(get("mask_1x1xSxS_bk0").reshape(T, T))
    mask, mask_t = (np.ascontiguousarray(a).view(np.int32) for a in (mask, mask.T))
    arrays = {"x": np.ascontiguousarray(get("x")), "context": np.ascontiguousarray(get("ctx_1024")),
              "mask": mask, "mask_t": mask_t,
              "weights": weights, "rows": rows, "vectors": vectors}
    nc = bacc.Bacc("TRN2", target_bir_lowering=False, num_devices=1, dynamic_dma_scratch_size=1024)
    args = [nc.dram_tensor(n, a.shape, mybir.dt.from_np(a.dtype), kind="ExternalInput").ap() for n, a in arrays.items()]
    args.append(nc.dram_tensor("out", (B, T, D), F32, kind="ExternalOutput").ap())
    attention_stack(nc, *args)
    r = run_bass_kernel_spmd(nc, [arrays], core_ids=[0])
    return r.results[0]["out"]
```
